# Optimizing a Trainium2 kernel written in Bass

```python
import numpy as np
import jax
import jax.numpy as jnp

def _softmax(x, axis=-1):
    return jax.nn.softmax(x, axis=axis)

def _gelu(x):
    return jax.nn.gelu(x, approximate=True)

def _silu(x):
    return jax.nn.silu(x)

def _sigmoid(x):
    return jax.nn.sigmoid(x)

def _layernorm(x, axis=-1, eps=1e-05):
    m = jnp.mean(x, axis=axis, keepdims=True)
    v = jnp.var(x, axis=axis, keepdims=True)
    return (x - m) / jnp.sqrt(v + eps)

def _scatter_add(tgt, idx, src, axis=0):
    return tgt.at[idx].add(src)

def _segment_sum(src, seg, n):
    return jax.ops.segment_sum(src, seg, n)
kernel_name = 'mk_lm_tower_d1_tok_ids512_r4_13993b'

def setup_inputs(seed: int=0):
    np.random.seed(seed)
    _w = jnp.asarray

    def _rec_inputs():
        import jax
        import jax.numpy as jnp
        _rk = jax.random.key(seed)
        x = jax.random.randint(jax.random.fold_in(_rk, 1), (2, 2048), 0, 16, jnp.int32)
        return x
    x = _rec_inputs()

    def _L0_tok_setup():
        import jax, jax.numpy as jnp
        import numpy as np
        VOCAB = 16
        D_MODEL = 128
        D_EMB = int(D_MODEL * 0.7)
        D_STFT = D_MODEL - D_EMB
        N_FFT = 64
        HOP = 64
        N_FREQ = N_FFT // 2 + 1
        B, L = (4, 2048)

        def _stft_mag(signal):
            pad = N_FFT // 2
            padded = jnp.pad(signal, ((0, 0), (pad, pad)), mode='reflect')
            n_frames = signal.shape[1] // HOP + 1
            idx = jnp.arange(n_frames)[:, None] * HOP + jnp.arange(N_FFT)[None, :]
            window = 0.5 - 0.5 * jnp.cos(2.0 * jnp.pi * jnp.arange(N_FFT) / N_FFT)
            frames = padded[:, idx] * window.astype(signal.dtype)
            return jnp.abs(jnp.fft.rfft(frames, axis=-1))
        key = jax.random.key(seed)
        k1, k2, k3, k4 = jax.random.split(key, 4)
        input_ids = jax.random.randint(k1, (B, L), 0, VOCAB)
        emb_table = jax.random.normal(k2, (VOCAB, D_EMB), dtype=jnp.float32) * 0.02
        proj_w = jax.random.normal(k3, (VOCAB * N_FREQ, D_STFT), dtype=jnp.float32) * 0.02
        proj_b = jnp.zeros((D_STFT,), dtype=jnp.float32)
        return {'input_ids': input_ids, 'emb_table': emb_table, 'proj_w': proj_w, 'proj_b': proj_b}
    _L0_tok_all = _L0_tok_setup()
    _L0_tok_in = {k: v for k, v in _L0_tok_all.items() if k in ('emb_table', 'proj_w', 'proj_b')}
    del _L0_tok_all

    def _L0_attn_setup():
        import jax, jax.numpy as jnp
        import numpy as np
        import math
        D_MODEL = 128
        N_HEADS = 8
        HEAD_DIM = D_MODEL // N_HEADS
        V_DIM = 2 * D_MODEL * N_HEADS
        LAYER_INDEX = 0
        LAMBDA_INIT = 0.8
        key = jax.random.key(seed)
        ks = jax.random.split(key, 12)
        B, S = (2, 512)
        s_in = 1.0 / math.sqrt(D_MODEL)
        s_v = 1.0 / math.sqrt(V_DIM)
        return {'x': jax.random.normal(ks[0], (B, S, D_MODEL), jnp.float32), 'Wqkv': jax.random.normal(ks[1], (D_MODEL, 2 * D_MODEL), jnp.float32) * s_in, 'bqkv': jnp.zeros((2 * D_MODEL,), jnp.float32), 'Wv': jax.random.normal(ks[2], (D_MODEL, V_DIM), jnp.float32) * s_in, 'bv': jnp.zeros((V_DIM,), jnp.float32), 'Wo': jax.random.normal(ks[3], (V_DIM, D_MODEL), jnp.float32) * s_v, 'bo': jnp.zeros((D_MODEL,), jnp.float32), 'lq1': jax.random.normal(ks[4], (HEAD_DIM,), jnp.float32) * 0.1, 'lk1': jax.random.normal(ks[5], (HEAD_DIM,), jnp.float32) * 0.1, 'lq2': jax.random.normal(ks[6], (HEAD_DIM,), jnp.float32) * 0.1, 'lk2': jax.random.normal(ks[7], (HEAD_DIM,), jnp.float32) * 0.1}
    _L0_attn_all = _L0_attn_setup()
    _L0_attn_in = {k: v for k, v in _L0_attn_all.items() if k in ('Wqkv', 'bqkv', 'Wv', 'bv', 'Wo', 'bo', 'lq1', 'lk1', 'lq2', 'lk2')}
    del _L0_attn_all

    def _L0_ffn_setup():
        import jax, jax.numpy as jnp
        import numpy as np
        G = 4
        EPG = 4
        E = 16
        KG = 2
        K = 2
        GTP = 0.9
        TP = 0.9
        SCALE = 1.0 / float(np.sqrt(G))

        def _routing_weights(xf, Wr, br, Wgate, bgate):
            N = xf.shape[0]
            gp = jax.nn.softmax(xf @ Wr + br, axis=-1)
            order = jnp.argsort(-gp, axis=-1)
            sp_k = jnp.take_along_axis(gp, order, axis=-1)[:, :KG]
            idx_k = order[:, :KG]
            act = jnp.cumsum(sp_k, axis=-1) <= GTP
            act = act.at[:, 0].set(True)
            mp = sp_k * act
            rn = mp / (jnp.sum(mp, axis=-1, keepdims=True) + 1e-09)
            w_group = jnp.zeros((N, G), xf.dtype).at[jnp.arange(N)[:, None], idx_k].set(rn)
            ep = jax.nn.softmax(jnp.einsum('nd,gde->nge', xf, Wgate) + bgate, axis=-1)
            eorder = jnp.argsort(-ep, axis=-1)
            esp = jnp.take_along_axis(ep, eorder, axis=-1)[:, :, :K]
            eidx = eorder[:, :, :K]
            eact = jnp.cumsum(esp, axis=-1) <= TP
            eact = eact.at[:, :, 0].set(True)
            emp = esp * eact
            ern = emp / (jnp.sum(emp, axis=-1, keepdims=True) + 1e-09)
            w_exp = jnp.zeros((N, G, EPG), xf.dtype).at[jnp.arange(N)[:, None, None], jnp.arange(G)[None, :, None], eidx].set(ern)
            return (w_group[:, :, None] * w_exp * SCALE).reshape(N, E)
        key = jax.random.key(seed)
        ks = jax.random.split(key, 6)
        B, T, D, H = (2, 256, 128, 512)
        x = jax.random.normal(ks[0], (B, T, D), jnp.float32)
        Wr = jax.random.normal(ks[1], (D, G), jnp.float32) * 0.02
        br = jnp.zeros((G,), jnp.float32)
        Wgate = jax.random.normal(ks[2], (G, D, EPG), jnp.float32) * 0.02
        bgate = jnp.zeros((G, EPG), jnp.float32)
        W1 = jax.random.normal(ks[3], (E, D, H), jnp.float32) * 0.02
        W3 = jax.random.normal(ks[4], (E, D, H), jnp.float32) * 0.02
        W2 = jax.random.normal(ks[5], (E, H, D), jnp.float32) * 0.02
        return {'x': x, 'Wr': Wr, 'br': br, 'Wgate': Wgate, 'bgate': bgate, 'W1': W1, 'W3': W3, 'W2': W2}
    _L0_ffn_all = _L0_ffn_setup()
    _L0_ffn_in = {k: v for k, v in _L0_ffn_all.items() if k in ('Wr', 'br', 'Wgate', 'bgate', 'W1', 'W3', 'W2')}
    del _L0_ffn_all
    return {'x': x, 'L0_tok_emb_table': _L0_tok_in['emb_table'], 'L0_tok_proj_w': _L0_tok_in['proj_w'], 'L0_tok_proj_b': _L0_tok_in['proj_b'], 'L0_attn_Wqkv': _L0_attn_in['Wqkv'], 'L0_attn_bqkv': _L0_attn_in['bqkv'], 'L0_attn_Wv': _L0_attn_in['Wv'], 'L0_attn_bv': _L0_attn_in['bv'], 'L0_attn_Wo': _L0_attn_in['Wo'], 'L0_attn_bo': _L0_attn_in['bo'], 'L0_attn_lq1': _L0_attn_in['lq1'], 'L0_attn_lk1': _L0_attn_in['lk1'], 'L0_attn_lq2': _L0_attn_in['lq2'], 'L0_attn_lk2': _L0_attn_in['lk2'], 'L0_ffn_Wr': _L0_ffn_in['Wr'], 'L0_ffn_br': _L0_ffn_in['br'], 'L0_ffn_Wgate': _L0_ffn_in['Wgate'], 'L0_ffn_bgate': _L0_ffn_in['bgate'], 'L0_ffn_W1': _L0_ffn_in['W1'], 'L0_ffn_W3': _L0_ffn_in['W3'], 'L0_ffn_W2': _L0_ffn_in['W2']}

def reference(x, L0_tok_emb_table, L0_tok_proj_w, L0_tok_proj_b, L0_attn_Wqkv, L0_attn_bqkv, L0_attn_Wv, L0_attn_bv, L0_attn_Wo, L0_attn_bo, L0_attn_lq1, L0_attn_lk1, L0_attn_lq2, L0_attn_lk2, L0_ffn_Wr, L0_ffn_br, L0_ffn_Wgate, L0_ffn_bgate, L0_ffn_W1, L0_ffn_W3, L0_ffn_W2):
    import jax
    import jax.numpy as jnp

    def _L0_tok_ref(input_ids, emb_table, proj_w, proj_b):
        import jax, jax.numpy as jnp
        import numpy as np
        VOCAB = 16
        D_MODEL = 128
        D_EMB = int(D_MODEL * 0.7)
        D_STFT = D_MODEL - D_EMB
        N_FFT = 64
        HOP = 64
        N_FREQ = N_FFT // 2 + 1
        B, L = (4, 2048)

        def _stft_mag(signal):
            pad = N_FFT // 2
            padded = jnp.pad(signal, ((0, 0), (pad, pad)), mode='reflect')
            n_frames = signal.shape[1] // HOP + 1
            idx = jnp.arange(n_frames)[:, None] * HOP + jnp.arange(N_FFT)[None, :]
            window = 0.5 - 0.5 * jnp.cos(2.0 * jnp.pi * jnp.arange(N_FFT) / N_FFT)
            frames = padded[:, idx] * window.astype(signal.dtype)
            return jnp.abs(jnp.fft.rfft(frames, axis=-1))
        b, seq_len = input_ids.shape
        word_embeds = emb_table[input_ids]
        onehot = jax.nn.one_hot(input_ids, VOCAB, dtype=jnp.float32)
        signal = onehot.transpose(0, 2, 1).reshape(b * VOCAB, seq_len)
        spec = _stft_mag(signal)
        n_frames = spec.shape[1]
        stft_mag = spec.reshape(b, VOCAB, n_frames, N_FREQ).transpose(0, 1, 3, 2)
        stft_to_up = stft_mag.transpose(0, 2, 1, 3).reshape(b, N_FREQ * VOCAB, n_frames)
        up_idx = jnp.arange(seq_len) * n_frames // seq_len
        stft_up = stft_to_up[:, :, up_idx]
        feats = stft_up.transpose(0, 2, 1)
        stft_enc = jnp.einsum('bli,io->blo', feats, proj_w) + proj_b
        return jnp.concatenate([word_embeds, stft_enc], axis=-1)

    def _L0_attn_ref(x, Wqkv, bqkv, Wv, bv, Wo, bo, lq1, lk1, lq2, lk2):
        import jax, jax.numpy as jnp
        import numpy as np
        import math
        D_MODEL = 128
        N_HEADS = 8
        HEAD_DIM = D_MODEL // N_HEADS
        V_DIM = 2 * D_MODEL * N_HEADS
        LAYER_INDEX = 0
        LAMBDA_INIT = 0.8
        qkv = x @ Wqkv + bqkv
        Q1, Q2, K1, K2 = jnp.split(qkv, 4, axis=-1)
        scale = 1.0 / math.sqrt(HEAD_DIM)
        attn1 = jax.nn.softmax(jnp.einsum('bqd,bkd->bqk', Q1, K1) * scale, axis=-1)
        attn2 = jax.nn.softmax(jnp.einsum('bqd,bkd->bqk', Q2, K2) * scale, axis=-1)
        lam = jnp.exp(jnp.sum(lq1 * lk1)) - jnp.exp(jnp.sum(lq2 * lk2)) + (LAMBDA_INIT - 0.6 * jnp.exp(jnp.asarray(-0.3 * LAYER_INDEX, jnp.float32)))
        diff_attn = attn1 - lam * attn2
        V = x @ Wv + bv
        out = jnp.einsum('bqk,bkv->bqv', diff_attn, V)
        return out @ Wo + bo

    def _L0_ffn_ref(x, Wr, br, Wgate, bgate, W1, W3, W2):
        import jax, jax.numpy as jnp
        import numpy as np
        G = 4
        EPG = 4
        E = 16
        KG = 2
        K = 2
        GTP = 0.9
        TP = 0.9
        SCALE = 1.0 / float(np.sqrt(G))

        def _routing_weights(xf, Wr, br, Wgate, bgate):
            N = xf.shape[0]
            gp = jax.nn.softmax(xf @ Wr + br, axis=-1)
            order = jnp.argsort(-gp, axis=-1)
            sp_k = jnp.take_along_axis(gp, order, axis=-1)[:, :KG]
            idx_k = order[:, :KG]
            act = jnp.cumsum(sp_k, axis=-1) <= GTP
            act = act.at[:, 0].set(True)
            mp = sp_k * act
            rn = mp / (jnp.sum(mp, axis=-1, keepdims=True) + 1e-09)
            w_group = jnp.zeros((N, G), xf.dtype).at[jnp.arange(N)[:, None], idx_k].set(rn)
            ep = jax.nn.softmax(jnp.einsum('nd,gde->nge', xf, Wgate) + bgate, axis=-1)
            eorder = jnp.argsort(-ep, axis=-1)
            esp = jnp.take_along_axis(ep, eorder, axis=-1)[:, :, :K]
            eidx = eorder[:, :, :K]
            eact = jnp.cumsum(esp, axis=-1) <= TP
            eact = eact.at[:, :, 0].set(True)
            emp = esp * eact
            ern = emp / (jnp.sum(emp, axis=-1, keepdims=True) + 1e-09)
            w_exp = jnp.zeros((N, G, EPG), xf.dtype).at[jnp.arange(N)[:, None, None], jnp.arange(G)[None, :, None], eidx].set(ern)
            return (w_group[:, :, None] * w_exp * SCALE).reshape(N, E)
        B, T, D = x.shape
        xf = x.reshape(-1, D)
        tw = _routing_weights(xf, Wr, br, Wgate, bgate)
        out = jnp.zeros_like(xf)
        for e in range(E):
            h = jax.nn.silu(xf @ W1[e]) * (xf @ W3[e])
            out = out + tw[:, e:e + 1] * (h @ W2[e])
        return out.reshape(B, T, D)
    h = _L0_tok_ref(x, L0_tok_emb_table, L0_tok_proj_w, L0_tok_proj_b)
    h = h + _L0_attn_ref(_layernorm(h, axis=-1), L0_attn_Wqkv, L0_attn_bqkv, L0_attn_Wv, L0_attn_bv, L0_attn_Wo, L0_attn_bo, L0_attn_lq1, L0_attn_lk1, L0_attn_lq2, L0_attn_lk2)
    h = h + _L0_ffn_ref(_layernorm(h, axis=-1), L0_ffn_Wr, L0_ffn_br, L0_ffn_Wgate, L0_ffn_bgate, L0_ffn_W1, L0_ffn_W3, L0_ffn_W2)
    return h

_drawn_inputs = setup_inputs


def setup_inputs(seed=0):
    import zlib

    import numpy as np

    out = dict(_drawn_inputs(seed))
    spreads = {'L0_tok_proj_b': (0.0, 0.1),
     'L0_attn_bqkv': (0.0, 0.351),
     'L0_attn_bv': (0.0, 0.1),
     'L0_attn_bo': (0.0, 0.1),
     'L0_ffn_br': (0.0, 0.8),
     'L0_ffn_bgate': (0.0, 0.8)}
    factors = {'L0_attn_lq2': 2.796,
     'L0_ffn_Wr': 8.0,
     'L0_ffn_Wgate': 8.0,
     'L0_ffn_W1': 8.0,
     'L0_ffn_W3': 8.0,
     'L0_ffn_W2': 8.0}
    for name, (base, spread) in spreads.items():
        noise = np.random.default_rng([zlib.crc32(name.encode()), seed]).standard_normal(out[name].shape)
        drawn = base * np.exp(spread * noise) if base else spread * noise
        out[name] = jnp.asarray(drawn.astype(out[name].dtype))
    for name, factor in factors.items():
        out[name] = (out[name] * factor).astype(out[name].dtype)
    return out
```

```python
from contextlib import ExitStack

import concourse.bass as bass
import numpy as np
from concourse import mybir

F32 = mybir.dt.float32
F32R = mybir.dt.float32r
BF16 = mybir.dt.bfloat16
I32 = mybir.dt.int32
ALU = mybir.AluOpType
ACT = mybir.ActivationFunctionType
X = mybir.AxisListType.X

B, L = 2, 2048
V = 16
D = 128
DE = 89
DS = D - DE
HOP = 64
NF = L // HOP + 1
NK = HOP // 2 + 1
BF = B * NF
C = BF * V
CB = NF * V
RT = 88
NT = C // RT
TB = CB // RT
NC3 = 352
N3 = C // NC3
KH = CB // 2
SPAN = -(-L // NF)
QD = 64
VD = 2048
VC = VD // 128
G, EPG = 4, 4
E = G * EPG
H = 512
HC = H // 128
SCALE = 0.25
LAM0 = 0.8 - 0.6
EPS = 1e-5
WIN = 3 * V
OT = B * L // 128
OHC = 16
STEPS = E * HC * N3
SE = HC * N3
NEG = -1.0e30

K_DFT = 0
K_VID = K_DFT + 2 * NK
K_PAD = K_VID + V
K_TIE = K_PAD + BF
K_REP = K_TIE + EPG * EPG
K_EARLY = K_REP + E
K_ID = K_EARLY
K_SEL = K_ID + 128
K_ALL = K_SEL + C


def shape_constants():
    k = np.zeros((128, K_ALL), np.float32)
    n = np.arange(HOP)
    window = 0.5 - 0.5 * np.cos(2 * np.pi * n / HOP)
    angle = 2 * np.pi * ((n[:, None] * np.arange(NK)[None, :]) % HOP) / HOP
    k[:HOP, K_DFT:K_DFT + NK] = window[:, None] * np.cos(angle)
    k[:HOP, K_DFT + NK:K_DFT + 2 * NK] = -window[:, None] * np.sin(angle)
    k[:, K_VID:K_VID + V] = np.arange(V)
    _, held = bucket_index()
    k[:SPAN, K_PAD:K_PAD + BF] = np.tile(np.where(held, 0.0, 100.0), (B, 1)).T
    i, j = np.divmod(np.arange(EPG * EPG), EPG)
    k[:, K_TIE:K_TIE + EPG * EPG] = j < i
    k[:3 * E, K_REP:K_REP + E] = (np.arange(3 * E)[:, None] % E) == np.arange(E)[None, :]
    k[:, K_ID:K_ID + 128] = np.eye(128)
    c = np.arange(C)
    k[c // V, K_SEL + c] = 1.0
    k[96 + c % V, K_SEL + c] = 1.0
    tok = np.arange(L)
    first = tok * NF // L - 2 * (tok // 128)
    pick = (np.arange(WIN)[:, None] - V * first[None, :]).astype(np.int32)
    return k, pick


def frame_index():
    at = np.arange(NF * HOP) - HOP // 2
    at = np.abs(at)
    at = np.where(at >= L, 2 * (L - 1) - at, at)
    return at.reshape(NF, HOP)


def bucket_index():
    up = np.arange(L) * NF // L
    at = np.zeros((NF, SPAN), np.int64)
    held = np.zeros((NF, SPAN), bool)
    for f in range(NF):
        t = np.flatnonzero(up == f)
        at[f, :len(t)] = t
        at[f, len(t):] = t[-1]
        held[f, :len(t)] = True
    return at, held


def build(nc, d, out):
    with ExitStack() as ctx:
        def sb(name, shape, dt=F32):
            return ctx.enter_context(nc.sbuf_tensor(name, shape, dt))

        def sem(name):
            return ctx.enter_context(nc.semaphore(name))

        region_a = sb("region_a", [128, 4 * C])
        region_b = sb("region_b", [128, 2 * C + VD])

        def carve(region, *shapes):
            at, views = 0, []
            for p, n in shapes:
                views.append(region[0:p, at:at + n])
                at += n
            assert at <= region.shape[1]
            return views

        sq, power, mag = carve(region_a, (NK, 2 * C), (NK, C), (NK, C))
        sq = sq.rearrange("k (m c) -> k m c", m=2)
        oh_frame, oh_span, wvT = carve(region_b, (HOP, C), (SPAN, C), (128, VD))
        wvT = wvT.rearrange("p (c n) -> p c n", c=VC)
        s_m, e_m, w_m, dif = carve(region_a, (RT, 2 * CB), (RT, 2 * CB), (RT, 2 * CB), (RT, CB))
        s_m, e_m, w_m = (r.rearrange("p (m c) -> p m c", m=2) for r in (s_m, e_m, w_m))
        NG = NT * (1 + G)
        lg, pr, rank, top1, top2, rn, gt, eq = carve(region_b, *[(RT, NG * 4)] * 6, *[(RT, NG * 16)] * 2)
        lg, pr, rank, top1, top2, rn = (r.rearrange("p (g e) -> p g e", e=4) for r in (lg, pr, rank, top1, top2, rn))
        gt, eq = (r.rearrange("p (g i j) -> p g i j", i=4, j=4) for r in (gt, eq))
        xs, act_h, gh = carve(region_a, (D, C), (128, 2 * NC3), (128, 3 * NC3))
        xs = xs.rearrange("p (n c) -> p n c", n=N3)
        act_h = act_h.rearrange("p (n c) -> p n c", n=2)
        gh = gh.rearrange("p (n c) -> p n c", n=3)

        kc = sb("kc", [128, K_ALL])
        ident = kc[:, K_ID:K_ID + 128]
        ids_wide = sb("ids_wide", [WIN, B * L], I32)
        frame_ids = sb("frame_ids", [HOP, BF], I32)
        span_ids = sb("span_ids", [SPAN, BF], I32)
        frame_f = sb("frame_f", [HOP, BF])
        span_f = sb("span_f", [SPAN, BF])
        ones = sb("ones", [128, 128])
        projw = sb("projw", [NK, V, DS])
        projb = sb("projb", [BF, DS])
        table = sb("table", [112, D])
        wqkv = sb("wqkv", [D, 4 * QD])
        bqk = sb("bqk", [D, 2])
        wv = sb("wv", [D, VD])
        wo = sb("wo", [128, VC, D])
        bvr = sb("bvr", [VC, 128])
        bvT = sb("bvT", [128, VC])
        wvo = sb("wvo", [D, D])
        bvo1 = sb("bvo1", [1, D])
        bvo = sb("bvo", [RT, D])
        bo = sb("bo", [RT, D])
        lqk = sb("lqk", [RT, 4, 16])
        ljunk = sb("ljunk", [RT, 2, 16])
        ldot = sb("ldot", [RT, 2])
        lexp = sb("lexp", [RT, 2])
        neglam = sb("neglam", [RT, 1])
        wrg = sb("wrg", [D, G + E])
        brg = sb("brg", [RT, G + E])
        hrow = sb("hrow", [RT, NT, D])
        hb = hrow
        st1 = sb("st1", [RT, NT, 6])
        mv1 = sb("mv1", [RT, NT, 2])
        zero = sb("zero", [128, 1])
        minus_half = sb("minus_half", [RT, NT])
        var1 = sb("var1", [RT, NT])
        var2 = sb("var2", [RT, 1])
        rstd1 = sb("rstd1", [RT, NT])
        xrow = sb("xrow", [RT, NT, D])
        xT = sb("xT", [D, C])
        qT = sb("qT", [D, C])
        kT = sb("kT", [D, C])
        vw = sb("vw", [RT, NT, D])
        cnt = sb("cnt", [RT, C])
        mask = sb("mask", [RT, C])
        mx = sb("mx", [RT, 2])
        nmx = sb("nmx", [RT, 2])
        den = sb("den", [RT, 2])
        rden = sb("rden", [RT, 2])
        ratio = sb("ratio", [RT, 1])
        difT = sb("difT", [RT, 2, 3 * RT])
        h2row = hrow
        st2 = sb("st2", [RT, 6])
        mv2 = sb("mv2", [RT, 2])
        rstd2 = sb("rstd2", [RT, 1])
        x2row = xrow
        xhT = sb("xhT", [D, 2, C])
        x2T, h2T = xhT[:, 0, :], xhT[:, 1, :]
        lmx = sb("lmx", [RT, NG])
        lsum = sb("lsum", [RT, NG])
        p1 = sb("p1", [RT, NG])
        p2 = sb("p2", [RT, NG])
        keep2 = sb("keep2", [RT, NG])
        tw = sb("tw", [RT, NT, E])
        tw3 = sb("tw3", [RT, NT, 3 * E], BF16)
        twT = sb("twT", [128, C], BF16)
        ident16 = sb("ident16", [128, 128], BF16)
        rep = sb("rep", [128, E, 128], BF16)
        x2hi = sb("x2hi", [D, C], F32R)
        x2lo = sb("x2lo", [D, C], F32R)
        xshi = sb("xshi", [D, 2, N3, NC3], F32R)
        xslo = sb("xslo", [D, 2, N3, NC3], F32R)
        wraw = sb("wraw", [128, 2, 3, H])
        whi = sb("whi", [128, 2, 3, H], F32R)
        wlo = sb("wlo", [128, 2, 3, H], F32R)
        ghi = sb("ghi", [128, 3, NC3], F32R)
        glo = sb("glo", [128, 3, NC3], F32R)
        pick = wv[0:WIN, :].bitcast(I32)
        yT = qT
        oh_out = ids_wide[:, :].bitcast(F32)
        yw = wo[0:WIN, 0:8, :].rearrange("p (s t) n -> p s t n", s=2)
        ow = wv[:, :].rearrange("p (s t n) -> p s t n", s=4, t=4)

        ps = ctx.enter_context(nc.psum_tensor("ps", [128, 8, 512], F32))

        names = """ids_in early_in spans_in sel_in proj_in projb_in emb_in wqkv_in bqk_in wv_in wo_in bv_in bo_in
        lam_in router_in rbias_in pick_in idswide_in table_clear zero_set twT_clear ones_set half_set var1_ready rstd1_ready var2_ready rstd2_ready whi_done xshi_done own rep_ready id16_ready power_ready cnt_saved bvo_saved
        ohf_ready ohs_ready spec_done sq_done mag_done enc_done table_ready hrow_done hrow_saved
        wvT_done wvT_saved bvT_done bvT_saved wvo_done wvo_saved bvo1_saved bvob_done
        cnt_done xrow_ready xT_done xT_saved qk_done q_saved k_saved vw_done vw_saved lexp_done
        sc_done sc_saved nmx_ready exp_done dif_ready difT_done difT_saved pv_done h2_ready x2_ready
        xh_done xh_saved logit_done logit_saved lexp2_ready lexp2_done tw_ready twT_done twT_saved
        y_seeded tws_done xs_done xs_split x2_split h1_done h3_done silu_done gh_done ghi_done glo_done y_done
        w_split y_saved yw_done yw_saved og_done ow_saved oh_done""".split()
        s = {n: sem(n) for n in names}
        out_done = [sem(f"out_done{i}") for i in range(4)]
        w_in = [sem(f"w_in{i}") for i in range(2)]

        w1 = d["w1"]
        w3 = d["w3"]
        w2 = d["w2"].rearrange("e (p c) n -> e p (c n)", c=HC)

        block = ctx.enter_context(nc.Block())

        @block.sync
        def _(sp):
            sp.dma_start(frame_ids[:, :], d["frame_ids"]).then_inc(s["ids_in"], 16)
            sp.dma_start(kc[:, 0:K_EARLY], d["kc"][:, 0:K_EARLY]).then_inc(s["early_in"], 16)
            sp.dma_start(projw[:, :, :], d["proj_w"].rearrange("(k v) o -> k v o", v=V)).then_inc(s["proj_in"], 16)
            sp.dma_start(projb[:, :], d["proj_b"].partition_broadcast(BF)).then_inc(s["projb_in"], 16)
            sp.dma_start(kc[:, K_EARLY:K_ALL], d["kc"][:, K_EARLY:K_ALL]).then_inc(s["sel_in"], 16)
            sp.wait_ge(s["table_clear"], 1)
            sp.dma_start(table[96:96 + V, 0:DE], d["emb"]).then_inc(s["emb_in"], 16)
            sp.dma_start(wo[:, :, :], d["wo"].rearrange("(c p) n -> p c n", p=128)).then_inc(s["wo_in"], 16)

            def load_expert(e, slot):
                sp.dma_start(wraw[:, slot, 0, :], w1[e]).then_inc(w_in[slot], 16)
                sp.dma_start(wraw[:, slot, 1, :], w3[e]).then_inc(w_in[slot], 16)
                sp.dma_start(wraw[:, slot, 2, :], w2[e]).then_inc(w_in[slot], 16)

            for e in range(2):
                load_expert(e, e)
            sp.wait_ge(s["wvT_done"], 4)
            sp.dma_start(pick, d["pick"]).then_inc(s["pick_in"], 16)
            with sp.Fori(1, E // 2) as pair:
                for slot in range(2):
                    sp.wait_ge(s["w_split"], pair * 2 + (slot - 1))
                    sp.dma_start(wraw[:, slot, 0, :], w1[bass.ds(pair * 2 + slot, 1)].rearrange("a p n -> (a p) n")).then_inc(w_in[slot], 16)
                    sp.dma_start(wraw[:, slot, 1, :], w3[bass.ds(pair * 2 + slot, 1)].rearrange("a p n -> (a p) n")).then_inc(w_in[slot], 16)
                    sp.dma_start(wraw[:, slot, 2, :], w2[bass.ds(pair * 2 + slot, 1)].rearrange("a p n -> (a p) n")).then_inc(w_in[slot], 16)
            o_view = out.rearrange("b (g t p) n -> (b g) p t n", p=128, t=4)
            for g in range(OT // 4):
                sp.wait_ge(s["ow_saved"], g + 1)
                sp.dma_start(o_view[g], ow[:, g % 4, :, :]).then_inc(out_done[g % 4], 16)
            for q in out_done:
                sp.wait_ge(q, 16 * (OT // 16))

        @block.gpsimd
        def _(pool):
            pool.memset(table[:, :], 0.0).then_inc(s["table_clear"], 1)
            pool.memset(twT[:, :], 0.0).then_inc(s["twT_clear"], 1)
            pool.memset(zero[:, :], 0.0).then_inc(s["zero_set"], 1)
            pool.wait_ge(s["zero_set"], 1)
            pool.memset(ones[:, :], 1.0).then_inc(s["ones_set"], 1)

            pool.memset(minus_half[:, :], -0.5).then_inc(s["half_set"], 1)
            pool.wait_ge(s["half_set"], 1)
            pool.wait_ge(s["var1_ready"], 1)
            pool.tensor_tensor(rstd1[:, :], var1[:, :], minus_half[:, :], ALU.pow).then_inc(s["rstd1_ready"], 1)

            def split_weights(e, slot):
                for m in range(3):
                    if m < 2:
                        src = wraw[:, slot, m, :].rearrange("k (p c) -> k c p", c=HC)
                    else:
                        src = wraw[:, slot, m, :].rearrange("k (c p) -> k c p", c=HC)
                    hi = whi[:, slot, m, :].rearrange("k (c p) -> k c p", c=HC)
                    lo = wlo[:, slot, m, :].rearrange("k (c p) -> k c p", c=HC)
                    if m == 0:
                        pool.tensor_tensor(hi, src, zero[:, 0:1].unsqueeze(2).to_broadcast([128, HC, 128]),
                                           ALU.add).then_inc(s["whi_done"], 1)
                    else:
                        pool.tensor_copy(hi, src).then_inc(s["whi_done"], 1)
                    pool.wait_ge(s["whi_done"], e * 3 + (m + 1))
                    last = pool.tensor_tensor(lo, src, hi, ALU.subtract)
                last.then_inc(s["w_split"], 1)

            def split_columns(e, slot):
                for c in range(N3):
                    pool.wait_ge(s["half_set"], 1)
                    pool.wait_ge(s["xs_done"], e * N3 + (c + 1))
                    pool.tensor_copy(xshi[:, slot, c, :], xs[:, c, :]).then_inc(s["xshi_done"], 1)
                    pool.wait_ge(s["xshi_done"], e * N3 + (c + 1))
                    pool.tensor_tensor(xslo[:, slot, c, :], xs[:, c, :], xshi[:, slot, c, :],
                                       ALU.subtract).then_inc(s["xs_split"], 1)

            for e in range(2):
                pool.wait_ge(w_in[e], 48)
                split_weights(e, e)
            for t in range(NT):
                pool.wait_ge(s["var2_ready"], t + 1)
                pool.tensor_tensor(rstd2[:, :], var2[:, :], minus_half[:, 0:1], ALU.pow).then_inc(s["rstd2_ready"], 1)
            for e in range(2):
                split_columns(e, e)
            with pool.Fori(1, E // 2) as pair:
                for slot in range(2):
                    pool.wait_ge(w_in[slot], pair * 48 + 48)
                    pool.wait_ge(s["y_done"], pair * (2 * SE) + (slot - 1) * SE)
                    split_weights(pair * 2 + slot, slot)
                    split_columns(pair * 2 + slot, slot)

        @block.scalar
        def _(act):
            act.dma_start(span_ids[:, :], d["span_ids"]).then_inc(s["spans_in"], 16)
            act.dma_start(wqkv[:, :], d["wqkv"]).then_inc(s["wqkv_in"], 16)
            act.dma_start(wv[:, :], d["wv"]).then_inc(s["wv_in"], 16)
            act.dma_start(bqk[:, :], d["bqkv"].rearrange("(m p) -> p m", p=128),
                          allow_slow_non_contiguous=True).then_inc(s["bqk_in"], 16)
            act.dma_start(bvr[:, :], d["bv"].rearrange("(c p) -> c p", p=128)).then_inc(s["bv_in"], 16)
            act.dma_start(bo[:, :], d["bo"].partition_broadcast(RT)).then_inc(s["bo_in"], 16)
            for i, n in enumerate(("lq1", "lk1", "lq2", "lk2")):
                act.dma_start(lqk[:, i, :], d[n].partition_broadcast(RT)).then_inc(s["lam_in"], 16)
            act.dma_start(wrg[:, 0:G], d["wr"]).then_inc(s["router_in"], 16)
            act.dma_start(wrg[:, G:].rearrange("k (g e) -> k g e", g=G),
                          d["wgate"].rearrange("g k e -> k g e")).then_inc(s["router_in"], 16)
            act.dma_start(brg[:, 0:G], d["br"].partition_broadcast(RT)).then_inc(s["rbias_in"], 16)
            act.dma_start(brg[:, G:], d["bgate"].rearrange("g e -> (g e)").partition_broadcast(RT)).then_inc(s["rbias_in"], 16)
            act.dma_start(ids_wide[:, :], d["ids"].rearrange("b l -> (b l)").partition_broadcast(WIN)).then_inc(s["idswide_in"], 16)

            for m in range(2):
                act.wait_ge(s["spec_done"], m + 1)
                act.activation(sq[:, m, :].rearrange("k (n c) -> k n c", n=N3),
                               ps[0:NK, 3 * m:3 * m + 3, 0:NC3], ACT.Square).then_inc(s["sq_done"], 1)
            act.wait_ge(s["power_ready"], 1)
            act.activation(mag[:, :], power[:, :], ACT.Sqrt).then_inc(s["mag_done"], 1)
            for g in range(4):
                act.wait_ge(s["wvT_done"], g + 1)
                act.activation(wvT[:, 4 * g:4 * g + 4, :], ps[:, 3 + g, :].rearrange("p (t n) -> p t n", t=4),
                               ACT.Copy).then_inc(s["wvT_saved"], 1)
            for n in range(N3):
                act.wait_ge(s["xT_done"], n + 1)
                act.activation(xT[:, n * NC3:(n + 1) * NC3], ps[:, n, 0:NC3], ACT.Copy).then_inc(s["xT_saved"], 1)
            act.wait_ge(s["bqk_in"], 16)
            for n in range(N3):
                act.wait_ge(s["qk_done"], n + 1)
                act.activation(qT[:, n * NC3:(n + 1) * NC3], ps[:, 3 + n, 0:NC3], ACT.Identity,
                               bias=bqk[:, 0:1]).then_inc(s["q_saved"], 1)
            act.wait_ge(s["lexp_done"], 2)
            act.activation(lexp[:, :], ldot[:, :], ACT.Exp).then_inc(s["lexp_done"], 1)

            def save_turned(t):
                act.wait_ge(s["xh_done"], t + 1)
                act.activation(xhT[:, :, t * RT:(t + 1) * RT],
                               ps[:, 7, :].rearrange("p (m c) -> p m c", m=2)[:, :, 0:RT],
                               ACT.Copy).then_inc(s["xh_saved"], 1)

            for t in range(NT):
                for m in range(2):
                    act.wait_ge(s["nmx_ready"], 2 * t + m + 1)
                    act.activation(e_m[:, m, :], s_m[:, m, :], ACT.Exp, bias=nmx[:, m:m + 1],
                                   scale=SCALE).then_inc(s["exp_done"], 1)
                act.wait_ge(s["difT_done"], t + 1)
                act.activation(difT[:, :, :], ps[0:RT, 4:6, 0:3 * RT], ACT.Copy).then_inc(s["difT_saved"], 1)
                if t >= 1:
                    save_turned(t - 1)
            save_turned(NT - 1)
            act.wait_ge(s["xh_saved"], NT)
            act.activation(x2hi[:, :], x2T, ACT.Copy).then_inc(s["x2_split"], 1)
            act.wait_ge(s["lexp2_ready"], 1)
            act.activation(pr[:, :, :], lg[:, :, :], ACT.Exp).then_inc(s["lexp2_done"], 1)
            act.wait_ge(s["twT_done"], 1)
            act.wait_ge(s["twT_clear"], 1)
            act.activation(twT[0:3 * E, :].rearrange("e (m c) -> e m c", m=2),
                           ps[0:3 * E, 3:5, 0:CB // 2].bitcast(BF16), ACT.Copy).then_inc(s["twT_saved"], 1)

            def silu(step, k):
                act.wait_ge(s["h1_done"], step + 1)
                act.activation(act_h[:, k % 2, :], ps[:, 3 + 2 * (k % 2), 0:NC3], ACT.Silu).then_inc(s["silu_done"], 1)

            def high(step, k):
                act.wait_ge(s["gh_done"], step + 1)
                act.activation(ghi[:, k % 3, :], gh[:, k % 3, :], ACT.Copy).then_inc(s["ghi_done"], 1)

            silu(0, 0)
            with act.Fori(0, E // 2 - 1) as pair:
                for k in range(2 * SE):
                    silu(pair * (2 * SE) + (k + 1), k + 1)
                    high(pair * (2 * SE) + k, k)
            for k in range(2 * SE):
                if k + 1 < 2 * SE:
                    silu(STEPS - 2 * SE + k + 1, k + 1)
                high(STEPS - 2 * SE + k, k)
            for g in range(OT // 4):
                act.wait_ge(s["og_done"], g + 1)
                if g >= 4:
                    act.wait_ge(out_done[g % 4], 16 * (g // 4))
                act.activation(ow[:, g % 4, :, :], ps[:, 3 + g % 2, :].rearrange("p (t n) -> p t n", t=4),
                               ACT.Copy).then_inc(s["ow_saved"], 1)

        @block.tensor
        def _(pe):
            mm = pe.matmul
            pe.wait_ge(s["early_in"], 16)
            pe.wait_ge(s["ohf_ready"], 1)
            for m in range(2):
                for n in range(N3):
                    last = mm(ps[0:NK, 3 * m + n, 0:NC3], kc[0:HOP, K_DFT + m * NK:K_DFT + (m + 1) * NK],
                              oh_frame[:, n * NC3:(n + 1) * NC3], start=True, stop=True)
                last.then_inc(s["spec_done"], 1)
            pe.wait_ge(s["sel_in"], 16)
            pe.wait_ge(s["bv_in"], 16)
            pe.transpose(ps[:, 7, 0:VC], bvr[:, :], ident[0:VC, 0:VC]).then_inc(s["bvT_done"], 1)
            pe.wait_ge(s["proj_in"], 16)
            pe.wait_ge(s["mag_done"], 1)
            by_id = mag[:, :].rearrange("k (f v) -> k v f", v=V)
            for v in range(V):
                last = mm(ps[0:BF, 6, 0:DS], by_id[:, v, :], projw[:, v, :], start=(v == 0), stop=(v == V - 1))
            last.then_inc(s["enc_done"], 1)
            pe.wait_ge(s["emb_in"], 16)
            pe.wait_ge(s["table_ready"], 1)
            for t in range(NT):
                last = mm(ps[0:RT, t // 4, (t % 4) * D:(t % 4 + 1) * D],
                          kc[0:112, K_SEL + t * RT:K_SEL + (t + 1) * RT], table[:, :], start=True, stop=True)
                if t % 4 == 3:
                    last.then_inc(s["hrow_done"], 1)
            pe.wait_ge(s["wv_in"], 16)
            for c in range(VC):
                last = pe.transpose(ps[:, 3 + c // 4, (c % 4) * 128:(c % 4 + 1) * 128], wv[:, c * 128:(c + 1) * 128], ident)
                if c % 4 == 3:
                    last.then_inc(s["wvT_done"], 1)
            pe.wait_ge(s["wo_in"], 16)
            pe.wait_ge(s["bvT_saved"], 1)
            for c in range(VC):
                if c % 4 == 0:
                    pe.wait_ge(s["wvT_saved"], c // 4 + 1)
                mm(ps[:, 7, 0:D], wvT[:, c, :], wo[:, c, :], start=(c == 0), stop=(c == VC - 1))
            for c in range(VC):
                last = mm(ps[0:1, 7, 256:256 + D], bvT[:, c:c + 1], wo[:, c, :], start=False, stop=(c == VC - 1),
                          skip_group_check=True)
            last.then_inc(s["wvo_done"], 1)
            pe.wait_ge(s["ohs_ready"], 1)
            pe.wait_ge(s["ones_set"], 1)
            for n in range(N3):
                last = mm(ps[0:RT, 3 + n, 0:NC3], ones[0:SPAN, 0:RT], oh_span[:, n * NC3:(n + 1) * NC3],
                          start=True, stop=True)
            last.then_inc(s["cnt_done"], 1)
            for t in range(NT):
                pe.wait_ge(s["xrow_ready"], t + 1)
                last = pe.transpose(ps[:, t // 4, (t % 4) * RT:(t % 4 + 1) * RT], xrow[:, t, :], ident[0:RT, 0:RT])
                if t % 4 == 3:
                    last.then_inc(s["xT_done"], 1)
            pe.wait_ge(s["bvo1_saved"], 1)
            mm(ps[0:RT, 6, 0:D], ones[0:1, 0:RT], bvo1[0:1, :], start=True, stop=True).then_inc(s["bvob_done"], 1)
            pe.wait_ge(s["wqkv_in"], 16)
            pe.wait_ge(s["cnt_saved"], 1)
            for m in range(2):
                for n in range(N3):
                    pe.wait_ge(s["xT_saved"], n + 1 if m == 0 else N3)
                    mm(ps[:, (3 if m == 0 else 0) + n, 0:NC3], wqkv[:, m * 128:(m + 1) * 128],
                       xT[:, n * NC3:(n + 1) * NC3], start=True, stop=True).then_inc(s["qk_done"], 1)
            pe.wait_ge(s["wvo_saved"], 1)
            for t in range(NT):
                if t == 0:
                    pe.wait_ge(s["bvo_saved"], 1)
                if t == 8:
                    pe.wait_ge(s["q_saved"], N3)
                last = mm(ps[0:RT, (6, 7, 3)[t // 4], (t % 4) * D:(t % 4 + 1) * D], xT[:, t * RT:(t + 1) * RT], wvo[:, :],
                          start=True, stop=True)
                if t % 4 == 3:
                    last.then_inc(s["vw_done"], 1)

            def scores(t):
                b = t // TB
                for m in range(2):
                    if t >= 1:
                        pe.wait_ge(s["sc_saved"], 2 * t - 1 + m)
                    for j in range(2):
                        last = mm(ps[0:RT, 2 * m + j, 0:KH], qT[m * QD:(m + 1) * QD, t * RT:(t + 1) * RT],
                                  kT[m * QD:(m + 1) * QD, b * CB + j * KH:b * CB + (j + 1) * KH], start=True, stop=True)
                    last.then_inc(s["sc_done"], 1)

            def turn_back(t):
                if t >= 1:
                    pe.wait_ge(s["xh_saved"], t)
                pe.wait_ge(s["x2_ready"], t + 1)
                pe.transpose(ps[:, 7, 0:RT], x2row[:, t, :], ident[0:RT, 0:RT])
                pe.transpose(ps[:, 7, 256:256 + RT], h2row[:, t, :], ident[0:RT, 0:RT]).then_inc(s["xh_done"], 1)

            pe.wait_ge(s["k_saved"], N3)
            pe.wait_ge(s["vw_saved"], 3)
            scores(0)
            for t in range(NT):
                if t + 1 < NT:
                    scores(t + 1)
                pe.wait_ge(s["dif_ready"], t + 1)
                if t >= 1:
                    pe.wait_ge(s["difT_saved"], t)
                for j in range(TB):
                    last = pe.transpose(ps[0:RT, 4 + j // 3, (j % 3) * RT:(j % 3 + 1) * RT],
                                        dif[:, j * RT:(j + 1) * RT], ident[0:RT, 0:RT])
                last.then_inc(s["difT_done"], 1)
                if t >= 1:
                    turn_back(t - 1)
                pe.wait_ge(s["difT_saved"], t + 1)
                if t >= 1:
                    pe.wait_ge(s["h2_ready"], t)
                for j in range(TB):
                    last = mm(ps[0:RT, 6, 0:D], difT[:, j // 3, (j % 3) * RT:(j % 3 + 1) * RT], vw[:, (t // TB) * TB + j, :],
                              start=(j == 0), stop=(j == TB - 1))
                last.then_inc(s["pv_done"], 1)
            turn_back(NT - 1)
            pe.wait_ge(s["router_in"], 32)
            pe.wait_ge(s["xh_saved"], NT)
            for t in range(NT):
                last = mm(ps[0:RT, 5, t * (G + E):(t + 1) * (G + E)], x2T[:, t * RT:(t + 1) * RT], wrg[:, :],
                          start=True, stop=True)
            last.then_inc(s["logit_done"], 1)
            for n in range(N3):
                mm(ps[:, n, 0:NC3], ident, h2T[:, n * NC3:(n + 1) * NC3], start=True, stop=True)
            pe.wait_ge(s["id16_ready"], 1)
            pe.wait_ge(s["tw_ready"], 1)
            for t in range(NT):
                last = pe.transpose(ps[0:3 * E, 3 + t // TB, 0:CB // 2].bitcast(BF16)[:, (t % TB) * RT:(t % TB + 1) * RT],
                                    tw3[:, t, :], ident16[0:RT, 0:RT])
            last.then_inc(s["twT_done"], 1)

            def spread(e, n):
                mm(ps[:, 7, 0:NC3], rep[:, bass.ds(e, 1), :].rearrange("k a n -> k (a n)"), twT[:, n * NC3:(n + 1) * NC3],
                   start=True, stop=True).then_inc(s["tws_done"], 1)

            def hidden(step, k, e):
                slot, j, n = (k // SE) % 2, (k % SE) // N3, k % N3
                pe_bank = 3 + 2 * (k % 2)
                if not (isinstance(step, int) and step < 2):
                    pe.wait_ge(s["gh_done"], step - 1)
                if k % SE == 0:
                    pe.wait_ge(s["w_split"], e + 1)
                c = slice(j * 128, (j + 1) * 128)
                cols = slice(n * NC3, (n + 1) * NC3)
                o = ps[:, pe_bank, 0:NC3]
                mm(o, whi[:, slot, 0, c], x2hi[:, cols], start=True, stop=False)
                mm(o, wlo[:, slot, 0, c], x2hi[:, cols], start=False, stop=False)
                mm(o, whi[:, slot, 0, c], x2lo[:, cols], start=False, stop=True).then_inc(s["h1_done"], 1)
                if j == 0:
                    pe.wait_ge(s["xs_split"], e * N3 + (n + 1))
                o = ps[:, pe_bank + 1, 0:NC3]
                mm(o, whi[:, slot, 1, c], xshi[:, slot, n, :], start=True, stop=False)
                mm(o, wlo[:, slot, 1, c], xshi[:, slot, n, :], start=False, stop=False)
                mm(o, whi[:, slot, 1, c], xslo[:, slot, n, :], start=False, stop=True).then_inc(s["h3_done"], 1)

            def back(step, k):
                slot, j, n = (k // SE) % 2, (k % SE) // N3, k % N3
                c = slice(j * 128, (j + 1) * 128)
                o = ps[:, n, 0:NC3]
                pe.wait_ge(s["ghi_done"], step + 1)
                mm(o, whi[:, slot, 2, c], ghi[:, k % 3, :], start=False, stop=False, skip_group_check=True)
                mm(o, wlo[:, slot, 2, c], ghi[:, k % 3, :], start=False, stop=False, skip_group_check=True)
                pe.wait_ge(s["glo_done"], step + 1)
                mm(o, whi[:, slot, 2, c], glo[:, k % 3, :], start=False, stop=True,
                   skip_group_check=True).then_inc(s["y_done"], 1)

            def pair_steps(base, e0, last):
                for k in range(2 * SE):
                    if k + 2 < 2 * SE or not last:
                        hidden(base + (k + 2), k + 2, e0 + (k + 2) // SE)
                    back(base + k, k)
                    e_in, r = divmod(k, SE)
                    if r in (1, 3, 5) and not (last and e_in == 1):
                        n = (r - 1) // 2
                        pe.wait_ge(s["xs_done"], (e0 + (e_in + 1)) * N3 + n)
                        spread(e0 + (e_in + 1), n)

            pe.wait_ge(s["twT_saved"], 1)
            pe.wait_ge(s["rep_ready"], 1)
            for n in range(N3):
                if n:
                    pe.wait_ge(s["xs_done"], n)
                spread(0, n)
            pe.wait_ge(s["x2_split"], 2)
            hidden(0, 0, 0)
            hidden(1, 1, 0)
            with pe.Fori(0, E // 2 - 1) as pair:
                pair_steps(pair * (2 * SE), pair * 2, False)
            pair_steps(STEPS - 2 * SE, E - 2, True)

            def windows(g):
                if g >= 2:
                    pe.wait_ge(s["yw_saved"], g - 1)
                for t in range(4):
                    tile = 4 * g + t
                    b, i = divmod(tile, OT // B)
                    at = b * CB + 2 * V * i
                    last = pe.transpose(ps[0:WIN, 5 + g % 2, t * D:(t + 1) * D], yT[:, at:at + WIN], ident)
                last.then_inc(s["yw_done"], 1)

            def picks(g):
                pe.wait_ge(s["yw_saved"], g + 1)
                if g >= 2:
                    pe.wait_ge(s["ow_saved"], g - 1)
                for t in range(4):
                    tile = 4 * g + t
                    last = mm(ps[:, 3 + g % 2, t * D:(t + 1) * D], oh_out[:, tile * 128:(tile + 1) * 128], yw[:, g % 2, t, :],
                              start=True, stop=True)
                last.then_inc(s["og_done"], 1)

            pe.wait_ge(s["y_saved"], N3)
            pe.wait_ge(s["oh_done"], OHC)
            windows(0)
            for g in range(OT // 4):
                if g + 1 < OT // 4:
                    windows(g + 1)
                picks(g)

        @block.vector
        def _(dve):
            made = [0]

            def link(ins):
                made[0] += 1
                ins.then_inc(s["own"], 1)
                dve.wait_ge(s["own"], made[0])

            dve.wait_ge(s["ids_in"], 16)
            link(dve.tensor_copy(frame_f[:, :], frame_ids[:, :]))
            dve.wait_ge(s["early_in"], 16)
            vid = kc[:, K_VID:K_VID + V].unsqueeze(1)
            dve.tensor_tensor(oh_frame[:, :].rearrange("n (f v) -> n f v", v=V),
                              frame_f[:, :].unsqueeze(2).to_broadcast([HOP, BF, V]),
                              vid[0:HOP].to_broadcast([HOP, BF, V]), ALU.is_equal).then_inc(s["ohf_ready"], 1)
            dve.wait_ge(s["spans_in"], 16)
            link(dve.tensor_tensor(span_f[:, :], span_ids[:, :], kc[0:SPAN, K_PAD:K_PAD + BF], ALU.add))
            dve.tensor_tensor(oh_span[:, :].rearrange("n (f v) -> n f v", v=V),
                              span_f[:, :].unsqueeze(2).to_broadcast([SPAN, BF, V]),
                              vid[0:SPAN].to_broadcast([SPAN, BF, V]), ALU.is_equal).then_inc(s["ohs_ready"], 1)
            dve.tensor_copy(rep[:, :, :], kc[:, K_REP:K_REP + E].unsqueeze(2).to_broadcast([128, E, 128]))\
               .then_inc(s["rep_ready"], 1)
            dve.wait_ge(s["lam_in"], 64)
            for i in range(2):
                dve.tensor_tensor_reduce(out=ljunk[:, i, :], in0=lqk[:, 2 * i, :], in1=lqk[:, 2 * i + 1, :], scale=1.0,
                                         scalar=0.0, op0=ALU.mult, op1=ALU.add,
                                         accum_out=ldot[:, i:i + 1]).then_inc(s["lexp_done"], 1)
            dve.wait_ge(s["sel_in"], 16)
            dve.tensor_copy(ident16[:, :], ident).then_inc(s["id16_ready"], 1)
            dve.wait_ge(s["bvT_done"], 1)
            dve.tensor_copy(bvT[:, :], ps[:, 7, 0:VC]).then_inc(s["bvT_saved"], 1)
            dve.wait_ge(s["sq_done"], 2)
            dve.tensor_tensor(power[:, :], sq[:, 0, :], sq[:, 1, :], ALU.add).then_inc(s["power_ready"], 1)
            dve.wait_ge(s["enc_done"], 1)
            dve.wait_ge(s["projb_in"], 16)
            dve.wait_ge(s["table_clear"], 1)
            dve.tensor_tensor(table[0:BF, DE:D], ps[0:BF, 6, 0:DS], projb[:, :], ALU.add).then_inc(s["table_ready"], 1)
            for g in range(3):
                dve.wait_ge(s["hrow_done"], g + 1)
                link(dve.tensor_copy(hrow[:, 4 * g:4 * g + 4, :], ps[0:RT, g, :].rearrange("p (t n) -> p t n", t=4)))
                for t in range(4 * g, 4 * g + 4):
                    last = dve.bn_stats(st1[:, t, :], hrow[:, t, :])
                link(last)
                for t in range(4 * g, 4 * g + 4):
                    last = dve.bn_aggr(mv1[:, t, :], st1[:, t, :])
                link(last)
            dve.tensor_scalar(var1[:, :], mv1[:, :, 1], EPS, None, ALU.add).then_inc(s["var1_ready"], 1)
            dve.wait_ge(s["rstd1_ready"], 1)
            for t in range(NT):
                dve.tensor_scalar(xrow[:, t, :], hrow[:, t, :], mv1[:, t, 0:1], rstd1[:, t:t + 1],
                                  ALU.subtract, ALU.mult).then_inc(s["xrow_ready"], 1)
            dve.wait_ge(s["wvo_done"], 1)
            dve.tensor_copy(bvo1[:, :], ps[0:1, 7, 256:256 + D]).then_inc(s["bvo1_saved"], 1)
            dve.tensor_copy(wvo[:, :], ps[:, 7, 0:D]).then_inc(s["wvo_saved"], 1)
            dve.wait_ge(s["cnt_done"], 1)
            dve.tensor_copy(cnt[:, :].rearrange("p (n c) -> p n c", n=N3), ps[0:RT, 3:6, 0:NC3]).then_inc(s["cnt_saved"], 1)
            dve.wait_ge(s["cnt_saved"], 1)
            link(dve.tensor_scalar(mask[:, :], cnt[:, :], 0.0, NEG, ALU.is_equal, ALU.mult))
            dve.wait_ge(s["bvob_done"], 1)
            dve.tensor_copy(bvo[:, :], ps[0:RT, 6, 0:D]).then_inc(s["bvo_saved"], 1)
            dve.wait_ge(s["bo_in"], 16)
            link(dve.tensor_tensor(hb[:, :, :], hrow[:, :, :], bo[:, :].unsqueeze(1).to_broadcast([RT, NT, D]), ALU.add))
            dve.wait_ge(s["lexp_done"], 3)
            link(dve.tensor_tensor(neglam[:, :], lexp[:, 1:2], lexp[:, 0:1], ALU.subtract))
            link(dve.tensor_scalar(neglam[:, :], neglam[:, :], -LAM0, None, ALU.add))
            dve.wait_ge(s["bqk_in"], 16)
            for n in range(N3):
                dve.wait_ge(s["qk_done"], N3 + n + 1)
                dve.tensor_scalar(kT[:, n * NC3:(n + 1) * NC3], ps[:, n, 0:NC3], bqk[:, 1:2], None,
                                  ALU.add).then_inc(s["k_saved"], 1)
            dve.wait_ge(s["bvo_saved"], 1)
            for g in range(3):
                dve.wait_ge(s["vw_done"], g + 1)
                dve.tensor_tensor(vw[:, 4 * g:4 * g + 4, :], ps[0:RT, (6, 7, 3)[g], :].rearrange("p (t n) -> p t n", t=4),
                                  bvo[:, :].unsqueeze(1).to_broadcast([RT, 4, D]), ALU.add).then_inc(s["vw_saved"], 1)

            def mask_max(t):
                b = t // TB
                keys = slice(b * CB, (b + 1) * CB)
                for m in range(2):
                    dve.wait_ge(s["sc_done"], 2 * t + m + 1)
                    if t >= 1:
                        dve.wait_ge(s["exp_done"], 2 * t - 1 + m)
                    dve.tensor_tensor_reduce(out=s_m[:, m, :].rearrange("p (j c) -> p j c", j=2),
                                             in0=ps[0:RT, 2 * m:2 * m + 2, 0:KH],
                                             in1=mask[:, keys].rearrange("p (j c) -> p j c", j=2),
                                             scale=1.0, scalar=-3.0e38, op0=ALU.add, op1=ALU.max,
                                             accum_out=mx[:, m:m + 1]).then_inc(s["sc_saved"], 1)
                    dve.wait_ge(s["sc_saved"], 2 * t + m + 1)
                    dve.tensor_scalar(nmx[:, m:m + 1], mx[:, m:m + 1], -SCALE, None, ALU.mult).then_inc(s["nmx_ready"], 1)

            def weigh(t):
                b = t // TB
                keys = slice(b * CB, (b + 1) * CB)
                for m in range(2):
                    dve.wait_ge(s["exp_done"], 2 * t + m + 1)
                    ins = dve.tensor_tensor_reduce(out=w_m[:, m, :], in0=e_m[:, m, :], in1=cnt[:, keys], scale=1.0,
                                                   scalar=0.0, op0=ALU.mult, op1=ALU.add, accum_out=den[:, m:m + 1])
                link(ins)
                link(dve.reciprocal(rden[:, :], den[:, :]))
                link(dve.scalar_tensor_tensor(out=ratio[:, :], in0=den[:, 0:1], scalar=neglam[:, 0:1], in1=rden[:, 1:2],
                                              op0=ALU.mult, op1=ALU.mult))
                if t >= 1:
                    dve.wait_ge(s["difT_done"], t)
                dve.scalar_tensor_tensor(out=dif[:, :], in0=w_m[:, 1, :], scalar=ratio[:, 0:1], in1=w_m[:, 0, :],
                                         op0=ALU.mult, op1=ALU.add).then_inc(s["dif_ready"], 1)

            def add_norm(t):
                dve.wait_ge(s["pv_done"], t + 1)
                dve.scalar_tensor_tensor(out=h2row[:, t, :], in0=ps[0:RT, 6, 0:D], scalar=rden[:, 0:1], in1=hb[:, t, :],
                                         op0=ALU.mult, op1=ALU.add).then_inc(s["h2_ready"], 1)
                dve.wait_ge(s["h2_ready"], t + 1)
                link(dve.bn_stats(st2[:, :], h2row[:, t, :]))
                link(dve.bn_aggr(mv2[:, :], st2[:, :]))
                dve.tensor_scalar(var2[:, :], mv2[:, 1:2], EPS, None, ALU.add).then_inc(s["var2_ready"], 1)
                dve.wait_ge(s["rstd2_ready"], t + 1)
                dve.tensor_scalar(x2row[:, t, :], h2row[:, t, :], mv2[:, 0:1], rstd2[:, 0:1],
                                  ALU.subtract, ALU.mult).then_inc(s["x2_ready"], 1)

            mask_max(0)
            for t in range(NT):
                weigh(t)
                if t + 1 < NT:
                    mask_max(t + 1)
                add_norm(t)
            dve.wait_ge(s["x2_split"], 1)
            dve.tensor_tensor(x2lo[:, :], x2T, x2hi[:, :], ALU.subtract).then_inc(s["x2_split"], 1)

            dve.wait_ge(s["logit_done"], 1)
            dve.wait_ge(s["rbias_in"], 32)
            by_tile = lg[:, :, :].rearrange("p (t a) e -> p t (a e)", t=NT)
            link(dve.tensor_tensor(by_tile, ps[0:RT, 5, 0:NT * (G + E)].rearrange("p (t a) -> p t a", t=NT),
                                   brg[:, :].unsqueeze(1).to_broadcast([RT, NT, G + E]), ALU.add))
            link(dve.tensor_reduce(lmx[:, :], lg[:, :, :], X, ALU.max))
            S3 = [RT, NG, 4]
            S4 = [RT, NG, 4, 4]
            dve.tensor_tensor(lg[:, :, :], lg[:, :, :], lmx[:, :].unsqueeze(2).to_broadcast(S3),
                              ALU.subtract).then_inc(s["lexp2_ready"], 1)
            dve.wait_ge(s["lexp2_done"], 1)
            link(dve.tensor_reduce(lsum[:, :], pr[:, :, :], X, ALU.add))
            link(dve.reciprocal(lsum[:, :], lsum[:, :]))
            link(dve.tensor_tensor(pr[:, :, :], pr[:, :, :], lsum[:, :].unsqueeze(2).to_broadcast(S3), ALU.mult))
            p_i = pr[:, :, :].unsqueeze(3).to_broadcast(S4)
            p_j = pr[:, :, :].unsqueeze(2).to_broadcast(S4)
            front = kc[0:RT, K_TIE:K_TIE + 16].rearrange("p (i j) -> p i j", i=4).unsqueeze(1).to_broadcast(S4)
            dve.tensor_tensor(gt[:, :, :, :], p_j, p_i, ALU.is_gt)
            link(dve.tensor_tensor(eq[:, :, :, :], p_j, p_i, ALU.is_equal))
            link(dve.tensor_tensor(eq[:, :, :, :], eq[:, :, :, :], front, ALU.mult))
            link(dve.tensor_tensor(gt[:, :, :, :], gt[:, :, :, :], eq[:, :, :, :], ALU.add))
            link(dve.tensor_reduce(rank[:, :, :], gt[:, :, :, :], X, ALU.add))
            dve.scalar_tensor_tensor(out=top1[:, :, :], in0=rank[:, :, :], scalar=0.0, in1=pr[:, :, :],
                                     op0=ALU.is_equal, op1=ALU.mult)
            link(dve.scalar_tensor_tensor(out=top2[:, :, :], in0=rank[:, :, :], scalar=1.0, in1=pr[:, :, :],
                                          op0=ALU.is_equal, op1=ALU.mult))
            dve.tensor_reduce(p1[:, :], top1[:, :, :], X, ALU.add)
            link(dve.tensor_reduce(p2[:, :], top2[:, :, :], X, ALU.add))
            link(dve.tensor_tensor(keep2[:, :], p1[:, :], p2[:, :], ALU.add))
            link(dve.tensor_scalar(keep2[:, :], keep2[:, :], 0.9, None, ALU.is_le))
            link(dve.tensor_tensor(p2[:, :], p2[:, :], keep2[:, :], ALU.mult))
            dve.tensor_tensor(top2[:, :, :], top2[:, :, :], keep2[:, :].unsqueeze(2).to_broadcast(S3), ALU.mult)
            link(dve.scalar_tensor_tensor(out=p1[:, :], in0=p1[:, :], scalar=1e-9, in1=p2[:, :], op0=ALU.add, op1=ALU.add))
            link(dve.reciprocal(p1[:, :], p1[:, :]))
            link(dve.tensor_tensor(rn[:, :, :], top1[:, :, :], top2[:, :, :], ALU.add))
            link(dve.tensor_tensor(rn[:, :, :], rn[:, :, :], p1[:, :].unsqueeze(2).to_broadcast(S3), ALU.mult))
            of = rn[:, :, :].rearrange("p (t a) e -> p t a e", t=NT)
            link(dve.tensor_scalar(rn[:, :, :].rearrange("p (t a) e -> p t a e", t=NT)[:, :, 0, :], of[:, :, 0, :],
                                   float(G) ** -0.5, None, ALU.mult))
            tw4 = tw[:, :, :].rearrange("p t (g e) -> p t g e", g=G)
            link(dve.tensor_tensor(tw4, of[:, :, 1:, :], of[:, :, 0, :].unsqueeze(3).to_broadcast([RT, NT, G, EPG]), ALU.mult))
            for part in range(3):
                o = tw3[:, :, part * E:(part + 1) * E]
                ins = dve.tensor_copy(o, tw[:, :, :])
                if part < 2:
                    link(ins)
                    link(dve.tensor_tensor(tw[:, :, :], tw[:, :, :], o, ALU.subtract))
                else:
                    ins.then_inc(s["tw_ready"], 1)

            def scale_columns(e, n):
                dve.wait_ge(s["tws_done"], e * N3 + (n + 1))
                if not (isinstance(e, int) and e == 0):
                    dve.wait_ge(s["xs_split"], (e - 1) * N3 + (n + 1))
                dve.tensor_tensor(xs[:, n, :], x2T[:, n * NC3:(n + 1) * NC3], ps[:, 7, 0:NC3],
                                  ALU.mult).then_inc(s["xs_done"], 1)

            def gate(step, k):
                dve.wait_ge(s["silu_done"], step + 1)
                dve.wait_ge(s["h3_done"], step + 1)
                dve.tensor_tensor(gh[:, k % 3, :], act_h[:, k % 2, :], ps[:, 4 + 2 * (k % 2), 0:NC3],
                                  ALU.mult).then_inc(s["gh_done"], 1)

            def low(step, k):
                dve.wait_ge(s["ghi_done"], step + 1)
                dve.tensor_tensor(glo[:, k % 3, :], gh[:, k % 3, :], ghi[:, k % 3, :],
                                  ALU.subtract).then_inc(s["glo_done"], 1)

            def pair_steps(base, e0, last):
                for k in range(2 * SE):
                    if k + 1 < 2 * SE or not last:
                        gate(base + (k + 1), k + 1)
                    low(base + k, k)
                    e_in, r = divmod(k, SE)
                    if r in (2, 4, 6) and not (last and e_in == 1):
                        scale_columns(e0 + (e_in + 1), (r - 2) // 2)
                    if last and k < OHC:
                        pick_classes(k)

            def pick_classes(i):
                at = i * (B * L // OHC)
                dve.tensor_tensor(oh_out[:, at:at + B * L // OHC], ids_wide[:, at:at + B * L // OHC],
                                  pick[:, at % L:at % L + B * L // OHC], ALU.is_equal).then_inc(s["oh_done"], 1)

            dve.wait_ge(s["pick_in"], 16)
            dve.wait_ge(s["idswide_in"], 16)
            for n in range(N3):
                scale_columns(0, n)
            gate(0, 0)
            with dve.Fori(0, E // 2 - 1) as pair:
                pair_steps(pair * (2 * SE), pair * 2, False)
            pair_steps(STEPS - 2 * SE, E - 2, True)
            for n in range(N3):
                dve.wait_ge(s["y_done"], STEPS)
                dve.tensor_copy(yT[:, n * NC3:(n + 1) * NC3], ps[:, n, 0:NC3]).then_inc(s["y_saved"], 1)
            for g in range(OT // 4):
                dve.wait_ge(s["yw_done"], g + 1)
                if g >= 2:
                    dve.wait_ge(s["og_done"], g - 1)
                dve.tensor_copy(yw[:, g % 2, :, :], ps[0:WIN, 5 + g % 2, :].rearrange("p (t n) -> p t n", t=4))\
                   .then_inc(s["yw_saved"], 1)


_INS = {
    "emb": "L0_tok_emb_table", "proj_w": "L0_tok_proj_w", "proj_b": "L0_tok_proj_b", "wqkv": "L0_attn_Wqkv",
    "bqkv": "L0_attn_bqkv", "wv": "L0_attn_Wv", "bv": "L0_attn_bv", "wo": "L0_attn_Wo", "bo": "L0_attn_bo",
    "lq1": "L0_attn_lq1", "lk1": "L0_attn_lk1", "lq2": "L0_attn_lq2", "lk2": "L0_attn_lk2", "wr": "L0_ffn_Wr",
    "br": "L0_ffn_br", "wgate": "L0_ffn_Wgate", "bgate": "L0_ffn_bgate", "w1": "L0_ffn_W1", "w3": "L0_ffn_W3",
    "w2": "L0_ffn_W2",
}


def kernel(**inputs):
    import concourse.bacc as _bacc
    from concourse.bass_utils import run_bass_kernel_spmd as _run

    ids = np.ascontiguousarray(inputs["x"])
    packed, pick = shape_constants()
    span_at, _ = bucket_index()
    laid = {n: np.ascontiguousarray(inputs[full]) for n, full in _INS.items()}
    laid["ids"] = ids
    laid["frame_ids"] = np.ascontiguousarray(ids[:, frame_index()].reshape(BF, HOP).T)
    laid["span_ids"] = np.ascontiguousarray(ids[:, span_at].reshape(BF, SPAN).T)
    laid["kc"] = packed
    laid["pick"] = pick

    nc = _bacc.Bacc("TRN2", target_bir_lowering=False, num_devices=1)
    arrays, d = {}, {}
    for n, a in laid.items():
        arrays[f"in_{n}_dram"] = a
        d[n] = nc.dram_tensor(f"in_{n}_dram", a.shape, mybir.dt.from_np(a.dtype), kind="ExternalInput").ap()
    out = nc.dram_tensor("out_dram", (B, L, D), F32, kind="ExternalOutput").ap()
    build(nc, d, out)
    r = _run(nc, [arrays], core_ids=[0])
    return r.results[0]["out_dram"]
```

```python
from contextlib import ExitStack

import concourse.bass as bass
import numpy as np
from concourse import mybir

F32 = mybir.dt.float32
F32R = mybir.dt.float32r
BF16 = mybir.dt.bfloat16
I32 = mybir.dt.int32
ALU = mybir.AluOpType
ACT = mybir.ActivationFunctionType
X = mybir.AxisListType.X

B, L = 2, 2048
V = 16
D = 128
DE = 89
DS = D - DE
HOP = 64
NF = L // HOP + 1
NK = HOP // 2 + 1
BF = B * NF
C = BF * V
CB = NF * V
RT = 88
NT = C // RT
TB = CB // RT
NC3 = 352
N3 = C // NC3
KH = CB // 2
SPAN = -(-L // NF)
QD = 64
VD = 2048
VC = VD // 128
G, EPG = 4, 4
E = G * EPG
H = 512
HC = H // 128
SCALE = 0.25
LAM0 = 0.8 - 0.6
EPS = 1e-5
WIN = 3 * V
OT = B * L // 128
OHC = 16
STEPS = E * HC * N3
SE = HC * N3
NEG = -1.0e30
WVT_BANKS = (7, 6, 7, 6)
QK_BANKS = (0, 1, 2, 3, 4, 5)
PROJECTIONS = [(n, part) for n in range(N3) for part in (0, 2, 1, 3)]
VW_BANKS = (7, 6, 5)

IM = 64
K_DFT = 0
K_VID = K_DFT + IM + NK
K_PAD = K_VID + V
K_TIE = K_PAD + BF
K_REP = K_TIE + EPG * EPG
K_EARLY = K_REP + E
K_ID = K_EARLY
K_SEL = K_ID + 128
K_ALL = K_SEL + C


def shape_constants():
    k = np.zeros((128, K_ALL), np.float32)
    n = np.arange(HOP)
    window = 0.5 - 0.5 * np.cos(2 * np.pi * n / HOP)
    angle = 2 * np.pi * ((n[:, None] * np.arange(NK)[None, :]) % HOP) / HOP
    for at, part in ((0, np.cos(angle)), (IM, -np.sin(angle))):
        dft = (window[:, None] * part).astype(np.float32)
        mantissa, exponent = np.frexp(dft)
        high = np.ldexp(np.round(mantissa * 4096) / 4096, exponent).astype(np.float32)
        k[:HOP, K_DFT + at:K_DFT + at + NK] = high
        k[HOP:, K_DFT + at:K_DFT + at + NK] = dft - high
    k[:, K_VID:K_VID + V] = np.arange(V)
    _, held = bucket_index()
    k[:SPAN, K_PAD:K_PAD + BF] = np.tile(np.where(held, 0.0, 100.0), (B, 1)).T
    i, j = np.divmod(np.arange(EPG * EPG), EPG)
    k[:, K_TIE:K_TIE + EPG * EPG] = j < i
    k[:3 * E, K_REP:K_REP + E] = (np.arange(3 * E)[:, None] % E) == np.arange(E)[None, :]
    k[:, K_ID:K_ID + 128] = np.eye(128)
    c = np.arange(C)
    k[c // V, K_SEL + c] = 1.0
    k[96 + c % V, K_SEL + c] = 1.0
    tok = np.arange(L)
    first = tok * NF // L - 2 * (tok // 128)
    pick = (np.arange(WIN)[:, None] - V * first[None, :]).astype(np.int32)
    return k, pick


def frame_index():
    at = np.arange(NF * HOP) - HOP // 2
    at = np.abs(at)
    at = np.where(at >= L, 2 * (L - 1) - at, at)
    return at.reshape(NF, HOP)


def bucket_index():
    up = np.arange(L) * NF // L
    at = np.zeros((NF, SPAN), np.int64)
    held = np.zeros((NF, SPAN), bool)
    for f in range(NF):
        t = np.flatnonzero(up == f)
        at[f, :len(t)] = t
        at[f, len(t):] = t[-1]
        held[f, :len(t)] = True
    return at, held


def build(nc, d, out):
    with ExitStack() as ctx:
        def sb(name, shape, dt=F32):
            return ctx.enter_context(nc.sbuf_tensor(name, shape, dt))

        def sem(name):
            return ctx.enter_context(nc.semaphore(name))

        region_a = sb("region_a", [128, 4 * C])
        region_b = sb("region_b", [128, 2 * C + VD])

        def carve(region, *shapes):
            at, views = 0, []
            for p, n in shapes:
                views.append(region[0:p, at:at + n])
                at += n
            assert at <= region.shape[1]
            return views

        whi = sb("whi", [128, 2, 3, H], F32R)
        sq, power, mag = carve(region_a, (NK, 2 * C), (NK, C), (NK, C))
        sq = sq.rearrange("k (m c) -> k m c", m=2)
        cnt1, absent, wvT = carve(region_b, (RT, C), (RT, C), (128, VD))
        oh_span = region_b[0:SPAN, 0:C]
        oh_span = oh_span.bitcast(BF16)[:, 0:C]
        wvT = wvT.rearrange("p (c n) -> p c n", c=VC)
        oh_frame = whi[:, 0, :, :].rearrange("p m h -> p (m h)")[:, 0:C]
        s_m, e_m = carve(region_a, (RT, 4 * CB), (RT, 4 * CB))
        s_m, e_m = (r.rearrange("p (b m c) -> p b m c", b=2, m=2) for r in (s_m, e_m))
        NG = NT * (1 + G)
        lg, pr, rank, top1, top2, rn, gt, eq = carve(region_b, *[(RT, NG * 4)] * 6, *[(RT, NG * 16)] * 2)
        lg, pr, rank, top1, top2, rn = (r.rearrange("p (g e) -> p g e", e=4) for r in (lg, pr, rank, top1, top2, rn))
        gt, eq = (r.rearrange("p (g i j) -> p g i j", i=4, j=4) for r in (gt, eq))
        xs, act_h, gh = carve(region_a, (D, C), (128, 2 * NC3), (128, 3 * NC3))
        xs = xs.rearrange("p (n c) -> p n c", n=N3)
        act_h = act_h.rearrange("p (n c) -> p n c", n=2)
        gh = gh.rearrange("p (n c) -> p n c", n=3)

        kc = sb("kc", [128, K_ALL])
        ident = kc[:, K_ID:K_ID + 128]
        ids_wide = sb("ids_wide", [WIN, B * L], I32)
        dft = sb("dft", [2 * HOP, IM + NK], F32R)
        frame_ids = sb("frame_ids", [2 * HOP, BF], I32)
        span_ids = sb("span_ids", [SPAN, BF], I32)
        frame_f = sb("frame_f", [2 * HOP, BF])
        span_f = sb("span_f", [SPAN, BF])
        ones = sb("ones", [SPAN, RT], BF16)
        projw = sb("projw", [NK, V, DS])
        projb = sb("projb", [BF, DS])
        table = sb("table", [112, D])
        wqkv = sb("wqkv", [D, 4, 2, QD])
        bqk = sb("bqk", [D, 4])
        wv = sb("wv", [D, VD])
        wo = sb("wo", [128, VC, D])
        bvr = sb("bvr", [VC, 128])
        bvT = sb("bvT", [128, VC])
        wvo = sb("wvo", [D, D])
        bvo1 = sb("bvo1", [D, RT])
        bvo = sb("bvo", [RT, D])
        bo = sb("bo", [RT, D])
        lqk = sb("lqk", [RT, 4, 16])
        ljunk = sb("ljunk", [RT, 2, 16])
        ldot = sb("ldot", [RT, 2])
        lexp = sb("lexp", [RT, 2])
        neglam = sb("neglam", [RT, 1])
        wrg = sb("wrg", [D, G + E])
        brg = sb("brg", [RT, G + E])
        hrow = sb("hrow", [RT, NT, D])
        hb = hrow
        st1 = sb("st1", [RT, NT, 6])
        mv1 = sb("mv1", [RT, NT, 2])
        zero = sb("zero", [128, 1])
        minus_half = sb("minus_half", [RT, NT])
        eps = sb("eps", [RT, 1])
        std1 = sb("std1", [RT, NT])
        var2 = sb("var2", [RT, NT])
        rstd1 = sb("rstd1", [RT, NT])
        xrow = sb("xrow", [RT, NT, D])
        xT = sb("xT", [D, C])
        vw = sb("vw", [RT, NT, D])
        weight = sb("weight", [RT, C])
        mx = sb("mx", [RT, NT, 2])
        nmx = sb("nmx", [RT, NT, 2])
        den = sb("den", [RT, NT, 2])
        rden = sb("rden", [RT, NT, 2])
        ratio = sb("ratio", [RT, NT])
        difT = sb("difT", [RT, 2, 3 * RT])
        h2row = hrow
        st2 = sb("st2", [RT, NT, 6])
        mv2 = sb("mv2", [RT, NT, 2])
        rstd2 = sb("rstd2", [RT, NT])
        x2row = xrow
        xhT = sb("xhT", [D, 2, C])
        x2T, h2T = xhT[:, 0, :], xhT[:, 1, :]
        lmx = sb("lmx", [RT, NG])
        lsum = sb("lsum", [RT, NG])
        p1 = sb("p1", [RT, NG])
        p2 = sb("p2", [RT, NG])
        keep2 = sb("keep2", [RT, NG])
        tw = sb("tw", [RT, NT, E])
        tw3 = sb("tw3", [RT, NT, 3 * E], BF16)
        twT = sb("twT", [128, C], BF16)
        ident16 = sb("ident16", [128, 128], BF16)
        rep = sb("rep", [128, E, 128], BF16)
        x2hi = sb("x2hi", [D, C], F32R)
        x2lo = sb("x2lo", [D, C], F32R)
        xshi = sb("xshi", [D, 2, N3, NC3], F32R)
        xslo = sb("xslo", [D, 2, N3, NC3], F32R)
        q_parts = (x2hi, x2lo)
        k_high, k_low = ([r[:, m, :, :].rearrange("k n c -> k (n c)") for m in range(2)] for r in (xshi, xslo))
        wraw = sb("wraw", [128, 2, 3, H])
        wlo = sb("wlo", [128, 2, 3, H], F32R)
        ghi = sb("ghi", [128, 3, NC3], F32R)
        glo = sb("glo", [128, 3, NC3], F32R)
        pick = wv[0:WIN, :].bitcast(I32)
        yT = xT
        oh_out = ids_wide[:, :].bitcast(F32)
        yw = wo[0:WIN, 0:8, :].rearrange("p (s t) n -> p s t n", s=2)
        ow = wv[:, :].rearrange("p (s t n) -> p s t n", s=4, t=4)

        ps = ctx.enter_context(nc.psum_tensor("ps", [128, 8, 512], F32))

        names = """ids_in early_in spans_in sel_in proj_in projb_in emb_in wqkv_in bqk_in wv_in wo_in bv_in bo_in
        lam_in router_in rbias_in pick_in idswide_in table_clear zero_set twT_clear ones_set half_set var1_ready eps_set dft_ready std1_ready var2_ready rstd2_ready whi_done xshi_done own rep_ready id16_ready power_ready cnt_saved bvo_saved
        ohf_ready ohs_ready spec_done sq_done mag_done enc_done table_ready hrow_done hrow_saved
        wvT_done wvT_saved bvT_done bvT_saved wvo_done wvo_saved bvo1_saved bvob_done
        cnt_done ln_done xrow_ready xT_done xT_saved qk_done qkhi_done qklo_done vw_done vw_saved lexp_done
        sc_done sc_saved nmx_ready exp_done dif_ready difT_done difT_saved pv_done h2_ready x2_ready
        xh_done xh_saved logit_done logit_saved lexp2_ready lexp2_done tw_ready twT_done twT_saved
        y_seeded tws_done xs_done xs_split x2hi_done x2lo_done h1_done h3_done silu_done gh_done ghi_done glo_done y_done
        w_split act_own hb_ready y_saved yw_done yw_saved og_done ow_saved oh_done""".split()
        s = {n: sem(n) for n in names}
        out_done = [sem(f"out_done{i}") for i in range(4)]
        w_in = [sem(f"w_in{i}") for i in range(2)]

        w1 = d["w1"]
        w3 = d["w3"]
        w2 = d["w2"].rearrange("e (p c) n -> e p (c n)", c=HC)

        block = ctx.enter_context(nc.Block())

        @block.sync
        def _(sp):
            sp.dma_start(frame_ids[:, :], d["frame_ids"]).then_inc(s["ids_in"], 16)
            sp.dma_start(kc[:, 0:K_EARLY], d["kc"][:, 0:K_EARLY]).then_inc(s["early_in"], 16)
            sp.dma_start(kc[:, K_EARLY:K_ALL], d["kc"][:, K_EARLY:K_ALL]).then_inc(s["sel_in"], 16)
            sp.dma_start(projw[:, :, :], d["proj_w"].rearrange("(k v) o -> k v o", v=V)).then_inc(s["proj_in"], 16)
            sp.dma_start(projb[:, :], d["proj_b"].partition_broadcast(BF)).then_inc(s["projb_in"], 16)
            sp.wait_ge(s["table_clear"], 1)
            sp.dma_start(table[96:96 + V, 0:DE], d["emb"]).then_inc(s["emb_in"], 16)
            sp.dma_start(wo[:, :, :], d["wo"].rearrange("(c p) n -> p c n", p=128)).then_inc(s["wo_in"], 16)

            def load_expert(e, slot):
                sp.dma_start(wraw[:, slot, 0, :], w1[e]).then_inc(w_in[slot], 16)
                sp.dma_start(wraw[:, slot, 1, :], w3[e]).then_inc(w_in[slot], 16)
                sp.dma_start(wraw[:, slot, 2, :], w2[e]).then_inc(w_in[slot], 16)

            for e in range(2):
                load_expert(e, e)
            sp.wait_ge(s["wvT_done"], 4)
            sp.dma_start(pick, d["pick"]).then_inc(s["pick_in"], 16)
            with sp.Fori(1, E // 2) as pair:
                for slot in range(2):
                    sp.wait_ge(s["w_split"], pair * 2 + (slot - 1))
                    sp.dma_start(wraw[:, slot, 0, :], w1[bass.ds(pair * 2 + slot, 1)].rearrange("a p n -> (a p) n")).then_inc(w_in[slot], 16)
                    sp.dma_start(wraw[:, slot, 1, :], w3[bass.ds(pair * 2 + slot, 1)].rearrange("a p n -> (a p) n")).then_inc(w_in[slot], 16)
                    sp.dma_start(wraw[:, slot, 2, :], w2[bass.ds(pair * 2 + slot, 1)].rearrange("a p n -> (a p) n")).then_inc(w_in[slot], 16)
            o_view = out.rearrange("b (g t p) n -> (b g) p t n", p=128, t=4)
            for g in range(OT // 4):
                sp.wait_ge(s["ow_saved"], g + 1)
                sp.dma_start(o_view[g], ow[:, g % 4, :, :]).then_inc(out_done[g % 4], 16)
            for q in out_done:
                sp.wait_ge(q, 16 * (OT // 16))

        @block.gpsimd
        def _(pool):
            pool.memset(table[:, :], 0.0).then_inc(s["table_clear"], 1)
            pool.memset(ones[:, :], 1.0).then_inc(s["ones_set"], 1)
            pool.wait_ge(s["early_in"], 16)
            pool.tensor_copy(dft[:, :], kc[:, K_DFT:K_DFT + IM + NK]).then_inc(s["dft_ready"], 1)
            pool.memset(twT[:, :], 0.0).then_inc(s["twT_clear"], 1)
            pool.memset(zero[:, :], 0.0).then_inc(s["zero_set"], 1)
            pool.memset(eps[:, :], EPS).then_inc(s["eps_set"], 1)
            pool.memset(minus_half[:, :], -0.5).then_inc(s["half_set"], 1)
            pool.wait_ge(s["half_set"], 1)
            pool.tensor_copy(rep[:, :, :], kc[:, K_REP:K_REP + E].unsqueeze(2).to_broadcast([128, E, 128]))\
                .then_inc(s["rep_ready"], 1)
            pool.wait_ge(s["sel_in"], 16)
            pool.tensor_copy(ident16[:, :], ident).then_inc(s["id16_ready"], 1)
            pool.wait_ge(s["bo_in"], 16)
            pool.wait_ge(s["xrow_ready"], NT)
            pool.tensor_tensor(hb[:, :, :], hrow[:, :, :], bo[:, :].unsqueeze(1).to_broadcast([RT, NT, D]), ALU.add)\
                .then_inc(s["hb_ready"], 1)

            def split_weights(e, slot):
                for m in range(3):
                    if m < 2:
                        src = wraw[:, slot, m, :].rearrange("k (p c) -> k c p", c=HC)
                    else:
                        src = wraw[:, slot, m, :].rearrange("k (c p) -> k c p", c=HC)
                    hi = whi[:, slot, m, :].rearrange("k (c p) -> k c p", c=HC)
                    lo = wlo[:, slot, m, :].rearrange("k (c p) -> k c p", c=HC)
                    if m == 0:
                        pool.tensor_tensor(hi, src, zero[:, 0:1].unsqueeze(2).to_broadcast([128, HC, 128]),
                                           ALU.add).then_inc(s["whi_done"], 1)
                    else:
                        pool.tensor_copy(hi, src).then_inc(s["whi_done"], 1)
                    pool.wait_ge(s["whi_done"], e * 3 + (m + 1))
                    last = pool.tensor_tensor(lo, src, hi, ALU.subtract)
                last.then_inc(s["w_split"], 1)

            def split_columns(e, slot):
                for c in range(N3):
                    pool.wait_ge(s["half_set"], 1)
                    pool.wait_ge(s["xs_done"], e * N3 + (c + 1))
                    pool.tensor_copy(xshi[:, slot, c, :], xs[:, c, :]).then_inc(s["xshi_done"], 1)
                    pool.wait_ge(s["xshi_done"], e * N3 + (c + 1))
                    pool.tensor_tensor(xslo[:, slot, c, :], xs[:, c, :], xshi[:, slot, c, :],
                                       ALU.subtract).then_inc(s["xs_split"], 1)

            for e in range(2):
                pool.wait_ge(w_in[e], 48)
                split_weights(e, e)
            for b in range(B):
                tiles = slice(b * TB, (b + 1) * TB)
                pool.wait_ge(s["var2_ready"], b + 1)
                pool.tensor_tensor(rstd2[:, tiles], var2[:, tiles], minus_half[:, tiles], ALU.pow)\
                    .then_inc(s["rstd2_ready"], 1)
            for b in range(B):
                cols = slice(b * CB, (b + 1) * CB)
                pool.wait_ge(s["x2hi_done"], b + 1)
                pool.tensor_tensor(x2lo[:, cols], x2T[:, cols], x2hi[:, cols], ALU.subtract).then_inc(s["x2lo_done"], 1)
            for e in range(2):
                split_columns(e, e)
            with pool.Fori(1, E // 2) as pair:
                for slot in range(2):
                    pool.wait_ge(w_in[slot], pair * 48 + 48)
                    pool.wait_ge(s["y_done"], pair * (2 * SE) + (slot - 1) * SE)
                    split_weights(pair * 2 + slot, slot)
                    split_columns(pair * 2 + slot, slot)

        @block.scalar
        def _(act):
            act.dma_start(span_ids[:, :], d["span_ids"]).then_inc(s["spans_in"], 16)
            act.dma_start(bvr[:, :], d["bv"].rearrange("(c p) -> c p", p=128)).then_inc(s["bv_in"], 16)
            act.dma_start(wv[:, :], d["wv"]).then_inc(s["wv_in"], 16)
            act.wait_ge(s["eps_set"], 1)
            act.activation(std1[:, 0:1], eps[:, :], ACT.Sqrt).then_inc(s["act_own"], 1)

            act.wait_ge(s["spec_done"], 1)
            for m in range(2):
                act.activation(sq[:, m, :].rearrange("k (n c) -> k n c", n=N3),
                               ps[m * IM:m * IM + NK, 0:N3, 0:NC3], ACT.Square).then_inc(s["sq_done"], 1)
            act.wait_ge(s["power_ready"], 1)
            act.activation(mag[:, :], power[:, :], ACT.Sqrt).then_inc(s["mag_done"], 1)
            for i in range(2):
                act.dma_start(wqkv[:, :, i, :], d["wqkv"].rearrange("k (m n) -> k m n", m=4)).then_inc(s["wqkv_in"], 16)
            for i in range(2):
                act.dma_start(bqk[i * QD:(i + 1) * QD, :], d["bqkv"].rearrange("(m p) -> p m", p=QD),
                              allow_slow_non_contiguous=True).then_inc(s["bqk_in"], 16)
            act.dma_start(bo[:, :], d["bo"].partition_broadcast(RT)).then_inc(s["bo_in"], 16)
            for i, n in enumerate(("lq1", "lk1", "lq2", "lk2")):
                act.dma_start(lqk[:, i, :], d[n].partition_broadcast(RT)).then_inc(s["lam_in"], 16)
            act.dma_start(wrg[:, 0:G], d["wr"]).then_inc(s["router_in"], 16)
            act.dma_start(wrg[:, G:].rearrange("k (g e) -> k g e", g=G),
                          d["wgate"].rearrange("g k e -> k g e")).then_inc(s["router_in"], 16)
            act.dma_start(brg[:, 0:G], d["br"].partition_broadcast(RT)).then_inc(s["rbias_in"], 16)
            act.dma_start(brg[:, G:], d["bgate"].rearrange("g e -> (g e)").partition_broadcast(RT)).then_inc(s["rbias_in"], 16)
            act.dma_start(ids_wide[:, :], d["ids"].rearrange("b l -> (b l)").partition_broadcast(WIN)).then_inc(s["idswide_in"], 16)

            def save_wvT(g):
                act.wait_ge(s["wvT_done"], g + 1)
                act.activation(wvT[:, 4 * g:4 * g + 4, :], ps[:, WVT_BANKS[g], :].rearrange("p (t n) -> p t n", t=4),
                               ACT.Copy).then_inc(s["wvT_saved"], 1)

            save_wvT(0)
            save_wvT(1)
            for g in range(3):
                act.wait_ge(s["hrow_done"], g + 1)
                act.activation(hrow[:, 4 * g:4 * g + 4, :], ps[0:RT, g, :].rearrange("p (t n) -> p t n", t=4),
                               ACT.Copy).then_inc(s["hrow_saved"], 1)
            act.wait_ge(s["act_own"], 1)
            for g in range(3):
                act.wait_ge(s["var1_ready"], g + 1)
                act.activation(std1[:, 4 * g:4 * g + 4], mv1[:, 4 * g:4 * g + 4, 1], ACT.Sqrt,
                               bias=eps[:, 0:1]).then_inc(s["std1_ready"], 1)
            save_wvT(2)
            save_wvT(3)
            act.wait_ge(s["cnt_saved"], 2)
            act.activation(weight[:, :], cnt1[:, :], ACT.Ln).then_inc(s["ln_done"], 1)
            act.wait_ge(s["lexp_done"], 2)
            act.activation(lexp[:, :], ldot[:, :], ACT.Exp).then_inc(s["lexp_done"], 1)
            for n in range(N3):
                act.wait_ge(s["xT_done"], n + 1)
                act.activation(xT[:, n * NC3:(n + 1) * NC3], ps[:, 3 + n, 0:NC3], ACT.Copy).then_inc(s["xT_saved"], 1)
            act.wait_ge(s["bqk_in"], 32)
            for i, (n, part) in enumerate(PROJECTIONS):
                act.wait_ge(s["qk_done"], i + 1)
                hi = (q_parts + tuple(k_high))[part]
                act.activation(hi[:, n * NC3:(n + 1) * NC3], ps[:, QK_BANKS[i % 6], 0:NC3], ACT.Identity,
                               bias=bqk[:, part:part + 1]).then_inc(s["qkhi_done"], 1)

            def exponentials(t):
                for m in range(2):
                    act.wait_ge(s["nmx_ready"], 2 * t + m + 1)
                    if t >= 2:
                        act.wait_ge(s["difT_done"], t - 1)
                    act.activation(e_m[:, t % 2, m, :], s_m[:, t % 2, m, :], ACT.Exp, bias=nmx[:, t, m:m + 1],
                                   scale=SCALE, accum_out=den[:, t, m:m + 1]).then_inc(s["exp_done"], 1)

            def save_turned(r):
                act.wait_ge(s["xh_done"], r + 1)
                act.activation(xhT[:, :, r * 2 * RT:(r + 1) * 2 * RT],
                               ps[:, 7, 0:4 * RT].rearrange("p (m c) -> p m c", m=2),
                               ACT.Copy).then_inc(s["xh_saved"], 1)

            exponentials(0)
            for t in range(NT):
                if t + 1 < NT:
                    exponentials(t + 1)
                act.wait_ge(s["difT_done"], t + 1)
                if t >= 1:
                    act.wait_ge(s["pv_done"], t)
                act.activation(difT[:, :, :], ps[0:RT, 4:6, 0:3 * RT], ACT.Copy).then_inc(s["difT_saved"], 1)
                if t >= NT - 3:
                    save_turned(t - (NT - 3))
            for b in range(B):
                if b == 1:
                    for r in range(3, 6):
                        save_turned(r)
                act.wait_ge(s["xh_saved"], 3 * (b + 1))
                act.activation(x2hi[:, b * CB:(b + 1) * CB], x2T[:, b * CB:(b + 1) * CB], ACT.Copy)\
                   .then_inc(s["x2hi_done"], 1)
            act.wait_ge(s["lexp2_ready"], 1)
            act.activation(pr[:, :, :], lg[:, :, :], ACT.Exp).then_inc(s["lexp2_done"], 1)
            act.wait_ge(s["twT_done"], 1)
            act.wait_ge(s["twT_clear"], 1)
            act.activation(twT[0:3 * E, :].rearrange("e (m c) -> e m c", m=2),
                           ps[0:3 * E, 3:5, 0:CB // 2].bitcast(BF16), ACT.Copy).then_inc(s["twT_saved"], 1)

            def silu(step, k):
                act.wait_ge(s["h1_done"], step + 1)
                act.activation(act_h[:, k % 2, :], ps[:, 3 + 2 * (k % 2), 0:NC3], ACT.Silu).then_inc(s["silu_done"], 1)

            def high(step, k):
                act.wait_ge(s["gh_done"], step + 1)
                act.activation(ghi[:, k % 3, :], gh[:, k % 3, :], ACT.Copy).then_inc(s["ghi_done"], 1)

            silu(0, 0)
            with act.Fori(0, E // 2 - 1) as pair:
                for k in range(2 * SE):
                    silu(pair * (2 * SE) + (k + 1), k + 1)
                    high(pair * (2 * SE) + k, k)
            for k in range(2 * SE):
                if k + 1 < 2 * SE:
                    silu(STEPS - 2 * SE + k + 1, k + 1)
                high(STEPS - 2 * SE + k, k)
            for g in range(OT // 4):
                act.wait_ge(s["og_done"], g + 1)
                if g >= 4:
                    act.wait_ge(out_done[g % 4], 16 * (g // 4))
                act.activation(ow[:, g % 4, :, :], ps[:, 3 + g % 2, :].rearrange("p (t n) -> p t n", t=4),
                               ACT.Copy).then_inc(s["ow_saved"], 1)

        @block.tensor
        def _(pe):
            mm = pe.matmul
            pe.wait_ge(s["dft_ready"], 1)
            pe.wait_ge(s["ohf_ready"], 1)
            for n in range(N3):
                last = mm(ps[0:IM + NK, n, 0:NC3], dft[:, :], oh_frame[:, n * NC3:(n + 1) * NC3], start=True, stop=True)
            last.then_inc(s["spec_done"], 1)
            pe.wait_ge(s["ohs_ready"], 1)
            pe.wait_ge(s["ones_set"], 1)
            for n in range(N3):
                last = mm(ps[0:RT, 3 + n, 0:NC3], ones[:, :], oh_span[:, n * NC3:(n + 1) * NC3],
                          start=True, stop=True)
            last.then_inc(s["cnt_done"], 1)
            pe.wait_ge(s["sel_in"], 16)
            pe.wait_ge(s["bv_in"], 16)
            pe.transpose(ps[:, 6, 0:VC], bvr[:, :], ident[0:VC, 0:VC]).then_inc(s["bvT_done"], 1)

            def turn_wv(g):
                if g == 1:
                    pe.wait_ge(s["bvT_saved"], 1)
                if g >= 2:
                    pe.wait_ge(s["wvT_saved"], g - 1)
                for c in range(4 * g, 4 * g + 4):
                    last = pe.transpose(ps[:, WVT_BANKS[g], (c % 4) * 128:(c % 4 + 1) * 128],
                                        wv[:, c * 128:(c + 1) * 128], ident)
                last.then_inc(s["wvT_done"], 1)

            pe.wait_ge(s["proj_in"], 16)
            pe.wait_ge(s["mag_done"], 1)
            by_id = mag[:, :].rearrange("k (f v) -> k v f", v=V)
            for v in range(V):
                last = mm(ps[0:BF, 0, 0:DS], by_id[:, v, :], projw[:, v, :], start=(v == 0), stop=(v == V - 1))
            last.then_inc(s["enc_done"], 1)
            pe.wait_ge(s["wv_in"], 16)
            turn_wv(0)
            turn_wv(1)
            pe.wait_ge(s["emb_in"], 16)
            pe.wait_ge(s["table_ready"], 1)
            for t in range(NT):
                last = mm(ps[0:RT, t // 4, (t % 4) * D:(t % 4 + 1) * D],
                          kc[0:112, K_SEL + t * RT:K_SEL + (t + 1) * RT], table[:, :], start=True, stop=True)
                if t % 4 == 3:
                    last.then_inc(s["hrow_done"], 1)
            turn_wv(2)
            turn_wv(3)
            pe.wait_ge(s["cnt_saved"], 2)
            for t in range(NT):
                pe.wait_ge(s["xrow_ready"], t + 1)
                last = pe.transpose(ps[:, 3 + t // 4, (t % 4) * RT:(t % 4 + 1) * RT], xrow[:, t, :], ident[0:RT, 0:RT])
                if t % 4 == 3:
                    last.then_inc(s["xT_done"], 1)
            pe.wait_ge(s["wo_in"], 16)
            pe.wait_ge(s["wvT_saved"], 4)
            for c in range(VC):
                mm(ps[:, 7, 0:D], wvT[:, c, :], wo[:, c, :], start=(c == 0), stop=(c == VC - 1))
            for c in range(VC):
                last = mm(ps[:, 7, 256:257], wo[:, c, :], bvT[:, c:c + 1], start=False, stop=(c == VC - 1),
                          skip_group_check=True)
            last.then_inc(s["wvo_done"], 1)
            pe.wait_ge(s["wqkv_in"], 32)
            for i, (n, part) in enumerate(PROJECTIONS):
                pe.wait_ge(s["xT_saved"], 1 if i < 4 else N3)
                if i == 0:
                    pe.wait_ge(s["hrow_saved"], 3)
                if i >= 6:
                    pe.wait_ge(s["qklo_done"], i - 5)
                mm(ps[:, QK_BANKS[i % 6], 0:NC3], wqkv[:, part, :, :].rearrange("k a n -> k (a n)"),
                   xT[:, n * NC3:(n + 1) * NC3], start=True, stop=True).then_inc(s["qk_done"], 1)
            pe.wait_ge(s["bvo1_saved"], 1)
            mm(ps[0:RT, 6, 0:D], bvo1[:, :], ident, start=True, stop=True).then_inc(s["bvob_done"], 1)

            def values():
                pe.wait_ge(s["wvo_saved"], 1)
                for t in range(NT):
                    if t == 4:
                        pe.wait_ge(s["bvo_saved"], 1)
                    last = mm(ps[0:RT, VW_BANKS[t // 4], (t % 4) * D:(t % 4 + 1) * D], xT[:, t * RT:(t + 1) * RT],
                              wvo[:, :], start=True, stop=True)
                    if t % 4 == 3:
                        last.then_inc(s["vw_done"], 1)

            def scores(t):
                b = t // TB
                for m in range(2):
                    if t >= 1:
                        pe.wait_ge(s["sc_saved"], 2 * t - 1 + m)
                    rows = slice(t * RT, (t + 1) * RT)
                    for j in range(2):
                        keys = slice(b * CB + j * KH, b * CB + (j + 1) * KH)
                        o = ps[0:RT, 2 * m + j, 0:KH]
                        mm(o, q_parts[m][:, rows], k_high[m][:, keys], start=True, stop=False)
                        last = mm(o, q_parts[m][:, rows], k_low[m][:, keys], start=False, stop=True)
                    last.then_inc(s["sc_done"], 1)

            def turn_back(r):
                if r >= 1:
                    pe.wait_ge(s["xh_saved"], r)
                pe.wait_ge(s["x2_ready"], 2 * r + 2)
                for i, rows in enumerate((x2row, h2row)):
                    for u in range(2):
                        last = pe.transpose(ps[:, 7, (2 * i + u) * RT:(2 * i + u + 1) * RT], rows[:, 2 * r + u, :],
                                            ident[0:RT, 0:RT])
                last.then_inc(s["xh_done"], 1)

            def times_values(t):
                pe.wait_ge(s["difT_saved"], t + 1)
                if t >= 1:
                    pe.wait_ge(s["h2_ready"], t)
                for j in range(TB):
                    last = mm(ps[0:RT, 6, 0:D], difT[:, j // 3, (j % 3) * RT:(j % 3 + 1) * RT], vw[:, (t // TB) * TB + j, :],
                              start=(j == 0), stop=(j == TB - 1))
                last.then_inc(s["pv_done"], 1)

            pe.wait_ge(s["qklo_done"], 4 * N3)
            scores(0)
            values()
            scores(1)
            for t in range(NT):
                if t >= 1:
                    times_values(t - 1)
                if t + 2 < NT:
                    scores(t + 2)
                if t == 0:
                    pe.wait_ge(s["vw_saved"], 3)
                pe.wait_ge(s["dif_ready"], t + 1)
                for j in range(TB):
                    last = pe.transpose(ps[0:RT, 4 + j // 3, (j % 3) * RT:(j % 3 + 1) * RT],
                                        e_m[:, t % 2, 0, j * RT:(j + 1) * RT], ident[0:RT, 0:RT])
                last.then_inc(s["difT_done"], 1)
                if t >= NT - 3:
                    turn_back(t - (NT - 3))
            times_values(NT - 1)
            for r in range(3, 6):
                turn_back(r)
            pe.wait_ge(s["router_in"], 32)
            pe.wait_ge(s["xh_saved"], 6)
            for t in range(NT):
                last = mm(ps[0:RT, 5, t * (G + E):(t + 1) * (G + E)], x2T[:, t * RT:(t + 1) * RT], wrg[:, :],
                          start=True, stop=True)
            last.then_inc(s["logit_done"], 1)
            for n in range(N3):
                mm(ps[:, n, 0:NC3], ident, h2T[:, n * NC3:(n + 1) * NC3], start=True, stop=True)
            pe.wait_ge(s["id16_ready"], 1)
            pe.wait_ge(s["tw_ready"], 1)
            for t in range(NT):
                last = pe.transpose(ps[0:3 * E, 3 + t // TB, 0:CB // 2].bitcast(BF16)[:, (t % TB) * RT:(t % TB + 1) * RT],
                                    tw3[:, t, :], ident16[0:RT, 0:RT])
            last.then_inc(s["twT_done"], 1)

            def spread(e, n):
                mm(ps[:, 7, 0:NC3], rep[:, bass.ds(e, 1), :].rearrange("k a n -> k (a n)"), twT[:, n * NC3:(n + 1) * NC3],
                   start=True, stop=True).then_inc(s["tws_done"], 1)

            def hidden(step, k, e):
                slot, j, n = (k // SE) % 2, (k % SE) // N3, k % N3
                pe_bank = 3 + 2 * (k % 2)
                if not (isinstance(step, int) and step < 2):
                    pe.wait_ge(s["gh_done"], step - 1)
                if k % SE == 0:
                    pe.wait_ge(s["w_split"], e + 1)
                c = slice(j * 128, (j + 1) * 128)
                cols = slice(n * NC3, (n + 1) * NC3)
                o = ps[:, pe_bank, 0:NC3]
                mm(o, whi[:, slot, 0, c], x2hi[:, cols], start=True, stop=False)
                mm(o, wlo[:, slot, 0, c], x2hi[:, cols], start=False, stop=False)
                mm(o, whi[:, slot, 0, c], x2lo[:, cols], start=False, stop=True).then_inc(s["h1_done"], 1)
                if j == 0:
                    pe.wait_ge(s["xs_split"], e * N3 + (n + 1))
                o = ps[:, pe_bank + 1, 0:NC3]
                mm(o, whi[:, slot, 1, c], xshi[:, slot, n, :], start=True, stop=False)
                mm(o, wlo[:, slot, 1, c], xshi[:, slot, n, :], start=False, stop=False)
                mm(o, whi[:, slot, 1, c], xslo[:, slot, n, :], start=False, stop=True).then_inc(s["h3_done"], 1)

            def back(step, k):
                slot, j, n = (k // SE) % 2, (k % SE) // N3, k % N3
                c = slice(j * 128, (j + 1) * 128)
                o = ps[:, n, 0:NC3]
                pe.wait_ge(s["ghi_done"], step + 1)
                mm(o, whi[:, slot, 2, c], ghi[:, k % 3, :], start=False, stop=False, skip_group_check=True)
                mm(o, wlo[:, slot, 2, c], ghi[:, k % 3, :], start=False, stop=False, skip_group_check=True)
                pe.wait_ge(s["glo_done"], step + 1)
                mm(o, whi[:, slot, 2, c], glo[:, k % 3, :], start=False, stop=True,
                   skip_group_check=True).then_inc(s["y_done"], 1)

            def pair_steps(base, e0, last):
                for k in range(2 * SE):
                    if k + 2 < 2 * SE or not last:
                        hidden(base + (k + 2), k + 2, e0 + (k + 2) // SE)
                    back(base + k, k)
                    e_in, r = divmod(k, SE)
                    if r in (1, 3, 5) and not (last and e_in == 1):
                        n = (r - 1) // 2
                        pe.wait_ge(s["xs_done"], (e0 + (e_in + 1)) * N3 + n)
                        spread(e0 + (e_in + 1), n)

            pe.wait_ge(s["twT_saved"], 1)
            pe.wait_ge(s["rep_ready"], 1)
            for n in range(N3):
                if n:
                    pe.wait_ge(s["xs_done"], n)
                spread(0, n)
            pe.wait_ge(s["x2lo_done"], B)
            hidden(0, 0, 0)
            hidden(1, 1, 0)
            with pe.Fori(0, E // 2 - 1) as pair:
                pair_steps(pair * (2 * SE), pair * 2, False)
            pair_steps(STEPS - 2 * SE, E - 2, True)

            def windows(g):
                if g >= 2:
                    pe.wait_ge(s["yw_saved"], g - 1)
                for t in range(4):
                    tile = 4 * g + t
                    b, i = divmod(tile, OT // B)
                    at = b * CB + 2 * V * i
                    last = pe.transpose(ps[0:WIN, 5 + g % 2, t * D:(t + 1) * D], yT[:, at:at + WIN], ident)
                last.then_inc(s["yw_done"], 1)

            def picks(g):
                pe.wait_ge(s["yw_saved"], g + 1)
                if g >= 2:
                    pe.wait_ge(s["ow_saved"], g - 1)
                for t in range(4):
                    tile = 4 * g + t
                    last = mm(ps[:, 3 + g % 2, t * D:(t + 1) * D], oh_out[:, tile * 128:(tile + 1) * 128], yw[:, g % 2, t, :],
                              start=True, stop=True)
                last.then_inc(s["og_done"], 1)

            pe.wait_ge(s["y_saved"], N3)
            pe.wait_ge(s["oh_done"], OHC)
            windows(0)
            for g in range(OT // 4):
                if g + 1 < OT // 4:
                    windows(g + 1)
                picks(g)

        @block.vector
        def _(dve):
            made = [0]

            def link(ins):
                made[0] += 1
                ins.then_inc(s["own"], 1)
                dve.wait_ge(s["own"], made[0])

            dve.wait_ge(s["ids_in"], 16)
            link(dve.tensor_copy(frame_f[:, :], frame_ids[:, :]))
            dve.wait_ge(s["early_in"], 16)
            vid = kc[:, K_VID:K_VID + V].unsqueeze(1)
            dve.tensor_tensor(oh_frame[:, :].rearrange("n (f v) -> n f v", v=V),
                              frame_f[:, :].unsqueeze(2).to_broadcast([2 * HOP, BF, V]),
                              vid.to_broadcast([2 * HOP, BF, V]), ALU.is_equal).then_inc(s["ohf_ready"], 1)
            dve.wait_ge(s["spans_in"], 16)
            link(dve.tensor_tensor(span_f[:, :], span_ids[:, :], kc[0:SPAN, K_PAD:K_PAD + BF], ALU.add))
            dve.tensor_tensor(oh_span[:, :].rearrange("n (f v) -> n f v", v=V),
                              span_f[:, :].unsqueeze(2).to_broadcast([SPAN, BF, V]),
                              vid[0:SPAN].to_broadcast([SPAN, BF, V]), ALU.is_equal).then_inc(s["ohs_ready"], 1)
            dve.wait_ge(s["bvT_done"], 1)
            dve.tensor_copy(bvT[:, :], ps[:, 6, 0:VC]).then_inc(s["bvT_saved"], 1)
            dve.wait_ge(s["sq_done"], 2)
            dve.tensor_tensor(power[:, :], sq[:, 0, :], sq[:, 1, :], ALU.add).then_inc(s["power_ready"], 1)
            dve.wait_ge(s["cnt_done"], 1)
            counts = ps[0:RT, 3:6, 0:NC3]
            dve.tensor_scalar(cnt1[:, :].rearrange("p (n c) -> p n c", n=N3), counts, 1.0, None, ALU.max)\
               .then_inc(s["cnt_saved"], 1)
            dve.tensor_scalar(absent[:, :].rearrange("p (n c) -> p n c", n=N3), counts, 0.0, NEG, ALU.is_equal, ALU.mult)\
               .then_inc(s["cnt_saved"], 1)
            dve.wait_ge(s["enc_done"], 1)
            dve.wait_ge(s["projb_in"], 16)
            dve.wait_ge(s["table_clear"], 1)
            dve.tensor_tensor(table[0:BF, DE:D], ps[0:BF, 0, 0:DS], projb[:, :], ALU.add).then_inc(s["table_ready"], 1)

            def h_statistics(g):
                dve.wait_ge(s["hrow_saved"], g + 1)
                for t in range(4 * g, 4 * g + 4):
                    last = dve.bn_stats(st1[:, t, :], hrow[:, t, :])
                link(last)
                for t in range(4 * g, 4 * g + 4):
                    last = dve.bn_aggr(mv1[:, t, :], st1[:, t, :])
                last.then_inc(s["var1_ready"], 1)

            def h_normalize(g):
                dve.wait_ge(s["std1_ready"], g + 1)
                link(dve.reciprocal(rstd1[:, 4 * g:4 * g + 4], std1[:, 4 * g:4 * g + 4]))
                for t in range(4 * g, 4 * g + 4):
                    dve.tensor_scalar(xrow[:, t, :], hrow[:, t, :], mv1[:, t, 0:1], rstd1[:, t:t + 1],
                                      ALU.subtract, ALU.mult).then_inc(s["xrow_ready"], 1)

            h_statistics(0)
            h_statistics(1)
            h_normalize(0)
            h_statistics(2)
            h_normalize(1)
            h_normalize(2)
            dve.wait_ge(s["lam_in"], 64)
            for i in range(2):
                dve.tensor_tensor_reduce(out=ljunk[:, i, :], in0=lqk[:, 2 * i, :], in1=lqk[:, 2 * i + 1, :], scale=1.0,
                                         scalar=0.0, op0=ALU.mult, op1=ALU.add,
                                         accum_out=ldot[:, i:i + 1]).then_inc(s["lexp_done"], 1)
            dve.wait_ge(s["wvo_done"], 1)
            dve.tensor_copy(bvo1[:, :], ps[:, 7, 256:257].to_broadcast([D, RT])).then_inc(s["bvo1_saved"], 1)
            dve.tensor_copy(wvo[:, :], ps[:, 7, 0:D]).then_inc(s["wvo_saved"], 1)
            dve.wait_ge(s["ln_done"], 1)
            link(dve.scalar_tensor_tensor(out=weight[:, :], in0=weight[:, :], scalar=1.0 / SCALE, in1=absent[:, :],
                                          op0=ALU.mult, op1=ALU.add))
            for i, (n, part) in enumerate(PROJECTIONS):
                cols = slice(n * NC3, (n + 1) * NC3)
                rows = slice(QD, 128) if part < 2 else slice(0, 128)
                hi = (q_parts + tuple(k_high))[part]
                lo = (q_parts + tuple(k_low))[part]
                dve.wait_ge(s["qkhi_done"], i + 1)
                dve.scalar_tensor_tensor(out=lo[rows, cols], in0=ps[rows, QK_BANKS[i % 6], 0:NC3],
                                         scalar=bqk[rows, part:part + 1], in1=hi[rows, cols],
                                         op0=ALU.add, op1=ALU.subtract).then_inc(s["qklo_done"], 1)

            def weigh_max(t):
                b = t // TB
                keys = slice(b * CB, (b + 1) * CB)
                for m in range(2):
                    dve.wait_ge(s["sc_done"], 2 * t + m + 1)
                    if t >= 2:
                        dve.wait_ge(s["exp_done"], 2 * t - 3 + m)
                    dve.tensor_tensor_reduce(out=s_m[:, t % 2, m, :].rearrange("p (j c) -> p j c", j=2),
                                             in0=ps[0:RT, 2 * m:2 * m + 2, 0:KH],
                                             in1=weight[:, keys].rearrange("p (j c) -> p j c", j=2),
                                             scale=1.0, scalar=-3.0e38, op0=ALU.add, op1=ALU.max,
                                             accum_out=mx[:, t, m:m + 1]).then_inc(s["sc_saved"], 1)
                for m in range(2):
                    dve.wait_ge(s["sc_saved"], 2 * t + m + 1)
                    dve.tensor_scalar(nmx[:, t, m:m + 1], mx[:, t, m:m + 1], -SCALE, None, ALU.mult)\
                       .then_inc(s["nmx_ready"], 1)

            def difference(t):
                dve.wait_ge(s["exp_done"], 2 * t + 2)
                link(dve.reciprocal(rden[:, t, :], den[:, t, :]))
                link(dve.scalar_tensor_tensor(out=ratio[:, t:t + 1], in0=den[:, t, 0:1], scalar=neglam[:, 0:1],
                                              in1=rden[:, t, 1:2], op0=ALU.mult, op1=ALU.mult))
                dve.scalar_tensor_tensor(out=e_m[:, t % 2, 0, :], in0=e_m[:, t % 2, 1, :], scalar=ratio[:, t:t + 1],
                                         in1=e_m[:, t % 2, 0, :], op0=ALU.mult, op1=ALU.add).then_inc(s["dif_ready"], 1)

            def residual(t):
                dve.wait_ge(s["pv_done"], t + 1)
                if t == 0:
                    dve.wait_ge(s["hb_ready"], 1)
                dve.scalar_tensor_tensor(out=h2row[:, t, :], in0=ps[0:RT, 6, 0:D], scalar=rden[:, t, 0:1], in1=hb[:, t, :],
                                         op0=ALU.mult, op1=ALU.add).then_inc(s["h2_ready"], 1)

            def statistics(b):
                tiles = range(b * TB, (b + 1) * TB)
                dve.wait_ge(s["h2_ready"], (b + 1) * TB)
                for t in tiles:
                    last = dve.bn_stats(st2[:, t, :], h2row[:, t, :])
                link(last)
                for t in tiles:
                    last = dve.bn_aggr(mv2[:, t, :], st2[:, t, :])
                link(last)
                dve.tensor_scalar(var2[:, b * TB:(b + 1) * TB], mv2[:, b * TB:(b + 1) * TB, 1], EPS, None,
                                  ALU.add).then_inc(s["var2_ready"], 1)

            def normalize(b):
                dve.wait_ge(s["rstd2_ready"], b + 1)
                for t in range(b * TB, (b + 1) * TB):
                    dve.tensor_scalar(x2row[:, t, :], h2row[:, t, :], mv2[:, t, 0:1], rstd2[:, t:t + 1],
                                      ALU.subtract, ALU.mult).then_inc(s["x2_ready"], 1)

            dve.wait_ge(s["bvob_done"], 1)
            dve.tensor_copy(bvo[:, :], ps[0:RT, 6, 0:D]).then_inc(s["bvo_saved"], 1)
            weigh_max(0)
            dve.wait_ge(s["bvo_saved"], 1)
            for g in range(3):
                dve.wait_ge(s["vw_done"], g + 1)
                dve.tensor_tensor(vw[:, 4 * g:4 * g + 4, :], ps[0:RT, VW_BANKS[g], :].rearrange("p (t n) -> p t n", t=4),
                                  bvo[:, :].unsqueeze(1).to_broadcast([RT, 4, D]), ALU.add).then_inc(s["vw_saved"], 1)
            dve.wait_ge(s["lexp_done"], 3)
            link(dve.tensor_tensor(neglam[:, :], lexp[:, 1:2], lexp[:, 0:1], ALU.subtract))
            link(dve.tensor_scalar(neglam[:, :], neglam[:, :], -LAM0, None, ALU.add))
            for t in range(NT):
                if t + 1 < NT:
                    weigh_max(t + 1)
                difference(t)
                if t >= 1:
                    residual(t - 1)
                if t == TB + 1:
                    statistics(0)
                if t == TB + 2:
                    normalize(0)
            residual(NT - 1)
            statistics(1)
            normalize(1)

            dve.wait_ge(s["logit_done"], 1)
            dve.wait_ge(s["rbias_in"], 32)
            by_tile = lg[:, :, :].rearrange("p (t a) e -> p t (a e)", t=NT)
            link(dve.tensor_tensor(by_tile, ps[0:RT, 5, 0:NT * (G + E)].rearrange("p (t a) -> p t a", t=NT),
                                   brg[:, :].unsqueeze(1).to_broadcast([RT, NT, G + E]), ALU.add))
            link(dve.tensor_reduce(lmx[:, :], lg[:, :, :], X, ALU.max))
            S3 = [RT, NG, 4]
            S4 = [RT, NG, 4, 4]
            dve.tensor_tensor(lg[:, :, :], lg[:, :, :], lmx[:, :].unsqueeze(2).to_broadcast(S3),
                              ALU.subtract).then_inc(s["lexp2_ready"], 1)
            dve.wait_ge(s["lexp2_done"], 1)
            link(dve.tensor_reduce(lsum[:, :], pr[:, :, :], X, ALU.add))
            link(dve.reciprocal(lsum[:, :], lsum[:, :]))
            link(dve.tensor_tensor(pr[:, :, :], pr[:, :, :], lsum[:, :].unsqueeze(2).to_broadcast(S3), ALU.mult))
            p_i = pr[:, :, :].unsqueeze(3).to_broadcast(S4)
            p_j = pr[:, :, :].unsqueeze(2).to_broadcast(S4)
            front = kc[0:RT, K_TIE:K_TIE + 16].rearrange("p (i j) -> p i j", i=4).unsqueeze(1).to_broadcast(S4)
            dve.tensor_tensor(gt[:, :, :, :], p_j, p_i, ALU.is_gt)
            link(dve.tensor_tensor(eq[:, :, :, :], p_j, p_i, ALU.is_equal))
            link(dve.tensor_tensor(eq[:, :, :, :], eq[:, :, :, :], front, ALU.mult))
            link(dve.tensor_tensor(gt[:, :, :, :], gt[:, :, :, :], eq[:, :, :, :], ALU.add))
            link(dve.tensor_reduce(rank[:, :, :], gt[:, :, :, :], X, ALU.add))
            dve.scalar_tensor_tensor(out=top1[:, :, :], in0=rank[:, :, :], scalar=0.0, in1=pr[:, :, :],
                                     op0=ALU.is_equal, op1=ALU.mult)
            link(dve.scalar_tensor_tensor(out=top2[:, :, :], in0=rank[:, :, :], scalar=1.0, in1=pr[:, :, :],
                                          op0=ALU.is_equal, op1=ALU.mult))
            dve.tensor_reduce(p1[:, :], top1[:, :, :], X, ALU.add)
            link(dve.tensor_reduce(p2[:, :], top2[:, :, :], X, ALU.add))
            link(dve.tensor_tensor(keep2[:, :], p1[:, :], p2[:, :], ALU.add))
            link(dve.tensor_scalar(keep2[:, :], keep2[:, :], 0.9, None, ALU.is_le))
            link(dve.tensor_tensor(p2[:, :], p2[:, :], keep2[:, :], ALU.mult))
            dve.tensor_tensor(top2[:, :, :], top2[:, :, :], keep2[:, :].unsqueeze(2).to_broadcast(S3), ALU.mult)
            link(dve.scalar_tensor_tensor(out=p1[:, :], in0=p1[:, :], scalar=1e-9, in1=p2[:, :], op0=ALU.add, op1=ALU.add))
            link(dve.reciprocal(p1[:, :], p1[:, :]))
            link(dve.tensor_tensor(rn[:, :, :], top1[:, :, :], top2[:, :, :], ALU.add))
            link(dve.tensor_tensor(rn[:, :, :], rn[:, :, :], p1[:, :].unsqueeze(2).to_broadcast(S3), ALU.mult))
            of = rn[:, :, :].rearrange("p (t a) e -> p t a e", t=NT)
            link(dve.tensor_scalar(rn[:, :, :].rearrange("p (t a) e -> p t a e", t=NT)[:, :, 0, :], of[:, :, 0, :],
                                   float(G) ** -0.5, None, ALU.mult))
            tw4 = tw[:, :, :].rearrange("p t (g e) -> p t g e", g=G)
            link(dve.tensor_tensor(tw4, of[:, :, 1:, :], of[:, :, 0, :].unsqueeze(3).to_broadcast([RT, NT, G, EPG]), ALU.mult))
            for part in range(3):
                o = tw3[:, :, part * E:(part + 1) * E]
                ins = dve.tensor_copy(o, tw[:, :, :])
                if part < 2:
                    link(ins)
                    link(dve.tensor_tensor(tw[:, :, :], tw[:, :, :], o, ALU.subtract))
                else:
                    ins.then_inc(s["tw_ready"], 1)

            def scale_columns(e, n):
                dve.wait_ge(s["tws_done"], e * N3 + (n + 1))
                if not (isinstance(e, int) and e == 0):
                    dve.wait_ge(s["xs_split"], (e - 1) * N3 + (n + 1))
                dve.tensor_tensor(xs[:, n, :], x2T[:, n * NC3:(n + 1) * NC3], ps[:, 7, 0:NC3],
                                  ALU.mult).then_inc(s["xs_done"], 1)

            def gate(step, k):
                dve.wait_ge(s["silu_done"], step + 1)
                dve.wait_ge(s["h3_done"], step + 1)
                dve.tensor_tensor(gh[:, k % 3, :], act_h[:, k % 2, :], ps[:, 4 + 2 * (k % 2), 0:NC3],
                                  ALU.mult).then_inc(s["gh_done"], 1)

            def low(step, k):
                dve.wait_ge(s["ghi_done"], step + 1)
                dve.tensor_tensor(glo[:, k % 3, :], gh[:, k % 3, :], ghi[:, k % 3, :],
                                  ALU.subtract).then_inc(s["glo_done"], 1)

            def pair_steps(base, e0, last):
                for k in range(2 * SE):
                    if k + 1 < 2 * SE or not last:
                        gate(base + (k + 1), k + 1)
                    low(base + k, k)
                    e_in, r = divmod(k, SE)
                    if r in (2, 4, 6) and not (last and e_in == 1):
                        scale_columns(e0 + (e_in + 1), (r - 2) // 2)
                    if last and k < OHC:
                        pick_classes(k)

            def pick_classes(i):
                at = i * (B * L // OHC)
                dve.tensor_tensor(oh_out[:, at:at + B * L // OHC], ids_wide[:, at:at + B * L // OHC],
                                  pick[:, at % L:at % L + B * L // OHC], ALU.is_equal).then_inc(s["oh_done"], 1)

            dve.wait_ge(s["pick_in"], 16)
            dve.wait_ge(s["idswide_in"], 16)
            for n in range(N3):
                scale_columns(0, n)
            gate(0, 0)
            with dve.Fori(0, E // 2 - 1) as pair:
                pair_steps(pair * (2 * SE), pair * 2, False)
            pair_steps(STEPS - 2 * SE, E - 2, True)
            for n in range(N3):
                dve.wait_ge(s["y_done"], STEPS)
                dve.tensor_copy(yT[:, n * NC3:(n + 1) * NC3], ps[:, n, 0:NC3]).then_inc(s["y_saved"], 1)
            for g in range(OT // 4):
                dve.wait_ge(s["yw_done"], g + 1)
                if g >= 2:
                    dve.wait_ge(s["og_done"], g - 1)
                dve.tensor_copy(yw[:, g % 2, :, :], ps[0:WIN, 5 + g % 2, :].rearrange("p (t n) -> p t n", t=4))\
                   .then_inc(s["yw_saved"], 1)


_INS = {
    "emb": "L0_tok_emb_table", "proj_w": "L0_tok_proj_w", "proj_b": "L0_tok_proj_b", "wqkv": "L0_attn_Wqkv",
    "bqkv": "L0_attn_bqkv", "wv": "L0_attn_Wv", "bv": "L0_attn_bv", "wo": "L0_attn_Wo", "bo": "L0_attn_bo",
    "lq1": "L0_attn_lq1", "lk1": "L0_attn_lk1", "lq2": "L0_attn_lq2", "lk2": "L0_attn_lk2", "wr": "L0_ffn_Wr",
    "br": "L0_ffn_br", "wgate": "L0_ffn_Wgate", "bgate": "L0_ffn_bgate", "w1": "L0_ffn_W1", "w3": "L0_ffn_W3",
    "w2": "L0_ffn_W2",
}


def kernel(**inputs):
    import concourse.bacc as _bacc
    from concourse.bass_utils import run_bass_kernel_spmd as _run

    ids = np.ascontiguousarray(inputs["x"])
    packed, pick = shape_constants()
    span_at, _ = bucket_index()
    laid = {n: np.ascontiguousarray(inputs[full]) for n, full in _INS.items()}
    laid["ids"] = ids
    frames = ids[:, frame_index()].reshape(BF, HOP).T
    laid["frame_ids"] = np.concatenate([frames, frames])
    laid["span_ids"] = np.ascontiguousarray(ids[:, span_at].reshape(BF, SPAN).T)
    laid["kc"] = packed
    laid["pick"] = pick

    nc = _bacc.Bacc("TRN2", target_bir_lowering=False, num_devices=1)
    arrays, d = {}, {}
    for n, a in laid.items():
        arrays[f"in_{n}_dram"] = a
        d[n] = nc.dram_tensor(f"in_{n}_dram", a.shape, mybir.dt.from_np(a.dtype), kind="ExternalInput").ap()
    out = nc.dram_tensor("out_dram", (B, L, D), F32, kind="ExternalOutput").ap()
    build(nc, d, out)
    r = _run(nc, [arrays], core_ids=[0])
    return r.results[0]["out_dram"]
```

```python
from contextlib import ExitStack

import concourse.bass as bass
import numpy as np
from concourse import mybir

F32 = mybir.dt.float32
F32R = mybir.dt.float32r
BF16 = mybir.dt.bfloat16
I32 = mybir.dt.int32
ALU = mybir.AluOpType
ACT = mybir.ActivationFunctionType
X = mybir.AxisListType.X

B, L = 2, 2048
V = 16
D = 128
DE = 89
DS = D - DE
HOP = 64
NF = L // HOP + 1
NK = HOP // 2 + 1
BF = B * NF
C = BF * V
CB = NF * V
RT = 88
NT = C // RT
TB = CB // RT
NC3 = 352
N3 = C // NC3
KH = CB // 2
SPAN = -(-L // NF)
QD = 64
VD = 2048
VC = VD // 128
G, EPG = 4, 4
E = G * EPG
H = 512
HC = H // 128
SCALE = 0.25
LAM0 = 0.8 - 0.6
EPS = 1e-5
WIN = 3 * V
OT = B * L // 128
OHC = 16
STEPS = E * HC * N3
SE = HC * N3
EARLY = SE
EARLY_BANKS = (3, 5, 4, 0, 1, 2)
IN_TURNING = HC
NEG = -1.0e30
WINDOW_BANKS = (7, 7, 7, 1, 7, 1, 7, 1)
PICK_BANKS = (0, 0, 0, 3, 0, 3, 0, 3)
WVT_BANKS = (7, 6, 7, 6)
QK_BANKS = (0, 1, 2, 3, 4, 5, 0, 1, 4, 5, 6, 7)
FIRST_QK = 10
PROJECTIONS = [(n, part) for n in range(N3) for part in (0, 2, 1, 3)]
VW_BANKS = (7, 6, 7)

IM = 64
K_DFT = 0
K_VID = K_DFT + IM + NK
K_PAD = K_VID + V
K_BEHIND = K_PAD + BF
K_REP = K_BEHIND + EPG
K_EARLY = K_REP + E
K_ID = K_EARLY
K_SEL = K_ID + 128
K_ALL = K_SEL + C


def shape_constants():
    k = np.zeros((128, K_ALL), np.float32)
    n = np.arange(HOP)
    window = 0.5 - 0.5 * np.cos(2 * np.pi * n / HOP)
    angle = 2 * np.pi * ((n[:, None] * np.arange(NK)[None, :]) % HOP) / HOP
    for at, part in ((0, np.cos(angle)), (IM, -np.sin(angle))):
        dft = (window[:, None] * part).astype(np.float32)
        mantissa, exponent = np.frexp(dft)
        high = np.ldexp(np.round(mantissa * 4096) / 4096, exponent).astype(np.float32)
        k[:HOP, K_DFT + at:K_DFT + at + NK] = high
        k[HOP:, K_DFT + at:K_DFT + at + NK] = dft - high
    k[:, K_VID:K_VID + V] = np.arange(V)
    _, held = bucket_index()
    k[:SPAN, K_PAD:K_PAD + BF] = np.tile(np.where(held, 0.0, 100.0), (B, 1)).T
    k[:, K_BEHIND:K_BEHIND + 3] = (3, 2, 1)
    k[:3 * E, K_REP:K_REP + E] = (np.arange(3 * E)[:, None] % E) == np.arange(E)[None, :]
    k[:, K_ID:K_ID + 128] = np.eye(128)
    c = np.arange(C)
    k[c // V, K_SEL + c] = 1.0
    k[96 + c % V, K_SEL + c] = 1.0
    tok = np.arange(L)
    first = tok * NF // L - 2 * (tok // 128)
    pick = (np.arange(WIN)[:, None] - V * first[None, :]).astype(np.int32)
    return k, pick


def frame_index():
    at = np.arange(NF * HOP) - HOP // 2
    at = np.abs(at)
    at = np.where(at >= L, 2 * (L - 1) - at, at)
    return at.reshape(NF, HOP)


def bucket_index():
    up = np.arange(L) * NF // L
    at = np.zeros((NF, SPAN), np.int64)
    held = np.zeros((NF, SPAN), bool)
    for f in range(NF):
        t = np.flatnonzero(up == f)
        at[f, :len(t)] = t
        at[f, len(t):] = t[-1]
        held[f, :len(t)] = True
    return at, held


def build(nc, d, out):
    with ExitStack() as ctx:
        def sb(name, shape, dt=F32):
            return ctx.enter_context(nc.sbuf_tensor(name, shape, dt))

        def sem(name):
            return ctx.enter_context(nc.semaphore(name))

        region_a = sb("region_a", [128, 4 * C])
        region_b = sb("region_b", [128, 2 * C + VD])

        def carve(region, *shapes):
            at, views = 0, []
            for p, n in shapes:
                views.append(region[0:p, at:at + n])
                at += n
            assert at <= region.shape[1]
            return views

        whi = sb("whi", [128, 2, 3, H], F32R)
        sq, power, mag = carve(region_a, (NK, 2 * C), (NK, C), (NK, C))
        sq = sq.rearrange("k (m c) -> k m c", m=2)
        cnt1, absent, wvT = carve(region_b, (RT, C), (RT, C), (128, VD))
        oh_span = region_b[0:SPAN, 0:C]
        oh_span = oh_span.bitcast(BF16)[:, 0:C]
        wvT = wvT.rearrange("p (c n) -> p c n", c=VC)
        oh_frame = whi[:, 0, :, :].rearrange("p m h -> p (m h)")[:, 0:C]
        bvw = region_a[:, 0:VD].rearrange("p (c n) -> p c n", c=VC)
        s_m, e_m = carve(region_a, (RT, 4 * CB), (RT, 4 * CB))
        s_m, e_m = (r.rearrange("p (b m c) -> p b m c", b=2, m=2) for r in (s_m, e_m))
        difT = region_b[0:RT, 0:2 * CB].rearrange("p (b j c) -> p b j c", b=2, j=2)
        NG = NT * (1 + G)
        lg, pr, rank, part2, part3, top1, top2, rn, *wins = carve(region_b[:, 2 * CB:], *[(RT, NG * 4)] * 8,
                                                                  *[(RT, NG * (4 + off)) for off in (1, 2, 3)])
        lg, pr, rank, part2, part3, top1, top2, rn = (r.rearrange("p (g e) -> p g e", e=4)
                                                      for r in (lg, pr, rank, part2, part3, top1, top2, rn))
        wins = [(w.rearrange("p (g e) -> p g e", g=NG), off) for off, w in enumerate(wins, 1)]
        xs, gh, act_h = carve(region_a, (D, C), (128, 3 * NC3), (128, 6 * NC3))
        xs = xs.rearrange("p (n c) -> p n c", n=N3)
        act_h = [act_h[:, i * NC3:(i + 1) * NC3] for i in range(6)]
        act_h += [region_b[:, i * NC3:(i + 1) * NC3] for i in range(3)]
        gh = gh.rearrange("p (n c) -> p n c", n=3)

        kc = sb("kc", [128, K_ALL])
        ident = kc[:, K_ID:K_ID + 128]
        ids_wide = sb("ids_wide", [WIN, B * L], I32)
        dft = sb("dft", [2 * HOP, IM + NK], F32R)
        frame_ids = sb("frame_ids", [2 * HOP, BF], I32)
        span_ids = sb("span_ids", [SPAN, BF], I32)
        frame_f = sb("frame_f", [2 * HOP, BF])
        span_f = sb("span_f", [SPAN, BF])
        ones = sb("ones", [SPAN, RT], BF16)
        projw = sb("projw", [NK, V, DS])
        projb = sb("projb", [BF, DS])
        table = sb("table", [112, D])
        wqkv = sb("wqkv", [D, 4, 2, QD])
        bqk = sb("bqk", [D, 4])
        wv = sb("wv", [D, VD])
        wo = sb("wo", [128, VC, D])
        bvr = sb("bvr", [VC, 128])
        bvT = sb("bvT", [128, VC])
        wvo = sb("wvo", [D, D])
        ones_f = sb("ones_f", [128, RT])
        bvo = sb("bvo", [RT, D])
        bo = sb("bo", [RT, D])
        lqk = sb("lqk", [RT, 4, 16])
        ljunk = sb("ljunk", [RT, 2, 16])
        ldot = sb("ldot", [RT, 2])
        lexp = sb("lexp", [RT, 2])
        neglam = sb("neglam", [RT, 1])
        wrg = sb("wrg", [D, G + E])
        brg = sb("brg", [RT, G + E])
        hrow = sb("hrow", [RT, NT, D])
        hb = hrow
        st1 = sb("st1", [RT, NT, 6])
        mv1 = sb("mv1", [RT, NT, 2])
        zero = sb("zero", [128, 1])
        minus_half = sb("minus_half", [RT, NT])
        eps = sb("eps", [RT, 1])
        std1 = sb("std1", [RT, NT])
        var2 = sb("var2", [RT, NT])
        rstd1 = sb("rstd1", [RT, NT])
        xrow = sb("xrow", [RT, NT, D])
        xT = sb("xT", [D, C])
        act_h += [xT[:, i * NC3:(i + 1) * NC3] for i in range(N3)]
        assert len(act_h) >= EARLY
        vw = sb("vw", [RT, NT, D])
        weight = sb("weight", [RT, C])
        mx = sb("mx", [RT, NT, 2])
        nmx = sb("nmx", [RT, NT, 2])
        den = sb("den", [RT, NT, 2])
        rden = sb("rden", [RT, NT, 2])
        ratio = sb("ratio", [RT, NT])
        attended = sb("attended", [RT, 2, D])
        h2row = hrow
        st2 = sb("st2", [RT, NT, 6])
        mv2 = sb("mv2", [RT, NT, 2])
        rstd2 = sb("rstd2", [RT, NT])
        x2row = xrow
        xhT = sb("xhT", [D, 2, C])
        x2T, h2T = xhT[:, 0, :], xhT[:, 1, :]
        lmx = sb("lmx", [RT, NG])
        lsum = sb("lsum", [RT, NG])
        p1 = sb("p1", [RT, NG])
        p2 = sb("p2", [RT, NG])
        keep2 = sb("keep2", [RT, NG])
        tw = sb("tw", [RT, NT, E])
        tw3 = sb("tw3", [RT, NT, 3 * E], BF16)
        twT = sb("twT", [128, C], BF16)
        ident16 = sb("ident16", [128, 128], BF16)
        rep = sb("rep", [128, E, 128], BF16)
        x2hi = sb("x2hi", [D, C], F32R)
        x2lo = sb("x2lo", [D, C], F32R)
        xshi = sb("xshi", [D, 2, N3, NC3], F32R)
        xslo = sb("xslo", [D, 2, N3, NC3], F32R)
        q_parts = (x2hi, x2lo)
        k_high, k_low = ([r[:, m, :, :].rearrange("k n c -> k (n c)") for m in range(2)] for r in (xshi, xslo))
        wraw = sb("wraw", [128, 2, 3, H])
        wlo = sb("wlo", [128, 2, 3, H], F32R)
        flat = wlo[:, :, :, :].rearrange("p s m h -> p (s m h)")
        select = flat[0:112, 0:C]
        table_hi, table_lo = (flat[0:112, C + i * D:C + (i + 1) * D] for i in range(2))
        ghi = sb("ghi", [128, 3, NC3], F32R)
        glo = sb("glo", [128, 3, NC3], F32R)
        pick = wv[0:WIN, :].bitcast(I32)
        yT = xT
        oh_out = ids_wide[:, :].bitcast(F32)
        yw = wo[0:WIN, 0:8, :].rearrange("p (s t) n -> p s t n", s=2)
        ow = wv[:, :].rearrange("p (s t n) -> p s t n", s=4, t=4)

        ps = ctx.enter_context(nc.psum_tensor("ps", [128, 8, 512], F32))

        names = """ids_in early_in spans_in sel_in proj_in projb_in emb_in wqkv_in bqk_in wv_in wo_in bv_in bo_in
        lam_in router_in rbias_in pick_in idswide_in table_clear zero_set twT_clear ones_set half_set
        var1_ready eps_set dft_ready std1_ready mv2_ready centred attended_ready var2_ready rstd2_ready
        whi_done xshi_done own rep_ready id16_ready power_ready cnt_saved bvo_saved ohf_ready ohs_ready
        spec_done sq_done mag_done enc_done select_ready table_high table_ready hrow_done hrow_saved
        wvT_done wvT_saved bvT_done bvT_saved wvo_done wvo_saved onesf_set pool_own bvob_done cnt_done
        ln_done xrow_ready xT_done xT_saved qk_done qkhi_done qklo_done vw_done vw_saved lexp_done sc_done
        sc_saved nmx_ready exp_done dif_ready difT_done difT_saved pv_done h2_ready x2_ready xh_done
        xh_saved logit_done logit_saved wins_set lexp2_ready lexp2_done tw_ready twT_done twT_saved tws_done
        xs_done xs_split x2hi_done x2lo_done h1_done h3_done silu_done gh_done ghi_done glo_done y_done
        w_split act_own hb_ready y_saved yw_done yw_saved og_done ow_saved oh_done""".split()
        s = {n: sem(n) for n in names}
        out_done = [sem(f"out_done{i}") for i in range(4)]
        w_in = [sem(f"w_in{i}") for i in range(2)]

        w1 = d["w1"]
        w3 = d["w3"]
        w2 = d["w2"].rearrange("e (p c) n -> e p (c n)", c=HC)

        block = ctx.enter_context(nc.Block())

        @block.sync
        def _(sp):
            sp.dma_start(frame_ids[:, :], d["frame_ids"]).then_inc(s["ids_in"], 16)
            sp.dma_start(kc[:, 0:K_EARLY], d["kc"][:, 0:K_EARLY]).then_inc(s["early_in"], 16)
            sp.dma_start(kc[:, K_EARLY:K_ALL], d["kc"][:, K_EARLY:K_ALL]).then_inc(s["sel_in"], 16)
            sp.dma_start(projw[:, :, :], d["proj_w"].rearrange("(k v) o -> k v o", v=V)).then_inc(s["proj_in"], 16)
            sp.dma_start(projb[:, :], d["proj_b"].partition_broadcast(BF)).then_inc(s["projb_in"], 16)
            sp.wait_ge(s["table_clear"], 1)
            sp.dma_start(table[96:96 + V, 0:DE], d["emb"]).then_inc(s["emb_in"], 16)
            sp.dma_start(wo[:, :, :], d["wo"].rearrange("(c p) n -> p c n", p=128)).then_inc(s["wo_in"], 16)
            for i in range(2):
                sp.dma_start(wqkv[:, :, i, :], d["wqkv"].rearrange("k (m n) -> k m n", m=4)).then_inc(s["wqkv_in"], 16)
            for i in range(2):
                sp.dma_start(bqk[i * QD:(i + 1) * QD, :], d["bqkv"].rearrange("(m p) -> p m", p=QD),
                              allow_slow_non_contiguous=True).then_inc(s["bqk_in"], 16)
            sp.dma_start(bo[:, :], d["bo"].partition_broadcast(RT)).then_inc(s["bo_in"], 16)
            for i, n in enumerate(("lq1", "lk1", "lq2", "lk2")):
                sp.dma_start(lqk[:, i, :], d[n].partition_broadcast(RT)).then_inc(s["lam_in"], 16)
            sp.dma_start(wrg[:, 0:G], d["wr"]).then_inc(s["router_in"], 16)
            sp.dma_start(wrg[:, G:].rearrange("k (g e) -> k g e", g=G),
                          d["wgate"].rearrange("g k e -> k g e")).then_inc(s["router_in"], 16)
            sp.dma_start(brg[:, 0:G], d["br"].partition_broadcast(RT)).then_inc(s["rbias_in"], 16)
            sp.dma_start(brg[:, G:], d["bgate"].rearrange("g e -> (g e)").partition_broadcast(RT)).then_inc(s["rbias_in"], 16)

            def load_expert(e, slot):
                sp.dma_start(wraw[:, slot, 0, :], w1[e]).then_inc(w_in[slot], 16)
                sp.dma_start(wraw[:, slot, 1, :], w3[e]).then_inc(w_in[slot], 16)
                sp.dma_start(wraw[:, slot, 2, :], w2[e]).then_inc(w_in[slot], 16)

            for e in range(2):
                load_expert(e, e)
            sp.wait_ge(s["wvT_done"], 4)
            sp.dma_start(pick, d["pick"]).then_inc(s["pick_in"], 16)
            sp.dma_start(ids_wide[:, :], d["ids"].rearrange("b l -> (b l)").partition_broadcast(WIN)).then_inc(s["idswide_in"], 16)
            with sp.Fori(1, E // 2) as pair:
                for slot in range(2):
                    sp.wait_ge(s["w_split"], pair * 2 + (slot - 1))
                    sp.dma_start(wraw[:, slot, 0, :], w1[bass.ds(pair * 2 + slot, 1)].rearrange("a p n -> (a p) n")).then_inc(w_in[slot], 16)
                    sp.dma_start(wraw[:, slot, 1, :], w3[bass.ds(pair * 2 + slot, 1)].rearrange("a p n -> (a p) n")).then_inc(w_in[slot], 16)
                    sp.dma_start(wraw[:, slot, 2, :], w2[bass.ds(pair * 2 + slot, 1)].rearrange("a p n -> (a p) n")).then_inc(w_in[slot], 16)
            o_view = out.rearrange("b (g t p) n -> (b g) p t n", p=128, t=4)
            for g in range(OT // 4):
                sp.wait_ge(s["ow_saved"], g + 1)
                sp.dma_start(o_view[g], ow[:, g % 4, :, :]).then_inc(out_done[g % 4], 16)
            for q in out_done:
                sp.wait_ge(q, 16 * (OT // 16))

        @block.gpsimd
        def _(pool):
            pool.memset(table[:, :], 0.0).then_inc(s["table_clear"], 1)
            pool.memset(ones[:, :], 1.0).then_inc(s["ones_set"], 1)
            pool.wait_ge(s["early_in"], 16)
            pool.tensor_copy(dft[:, :], kc[:, K_DFT:K_DFT + IM + NK]).then_inc(s["dft_ready"], 1)
            pool.memset(twT[:, :], 0.0).then_inc(s["twT_clear"], 1)
            pool.memset(zero[:, :], 0.0).then_inc(s["zero_set"], 1)
            pool.memset(eps[:, :], EPS).then_inc(s["eps_set"], 1)
            pool.memset(ones_f[:, :], 1.0).then_inc(s["onesf_set"], 1)
            pool.memset(minus_half[:, :], -0.5).then_inc(s["half_set"], 1)
            pool.wait_ge(s["half_set"], 1)
            pool.wait_ge(s["sel_in"], 16)
            pool.tensor_copy(select, kc[0:112, K_SEL:K_ALL]).then_inc(s["select_ready"], 1)
            pool.wait_ge(s["wo_in"], 16)
            pool.wait_ge(s["bvT_saved"], 1)
            pool.wait_ge(s["mag_done"], 1)
            pool.tensor_tensor(bvw[:, :, :], wo[:, :, :], bvT[:, :].unsqueeze(2).to_broadcast([128, VC, D]),
                               ALU.mult).then_inc(s["pool_own"], 1)
            n, made = VC // 2, 1
            while n:
                pool.wait_ge(s["pool_own"], made)
                pool.tensor_tensor(bvw[:, 0:n, :], bvw[:, 0:n, :], bvw[:, n:2 * n, :], ALU.add).then_inc(s["pool_own"], 1)
                n, made = n // 2, made + 1
            pool.tensor_copy(rep[:, :, :], kc[:, K_REP:K_REP + E].unsqueeze(2).to_broadcast([128, E, 128]))\
                .then_inc(s["rep_ready"], 1)
            pool.tensor_copy(ident16[:, :], ident).then_inc(s["id16_ready"], 1)
            pool.wait_ge(s["wvo_done"], 1)
            for w, off in wins:
                pool.memset(w[:, :, :], 0.0).then_inc(s["pool_own"], 1)
            pool.wait_ge(s["pool_own"], 8)
            pool.tensor_copy(wins[2][0][:, :, 0:3], kc[0:RT, K_BEHIND:K_BEHIND + 3].unsqueeze(1).to_broadcast([RT, NG, 3]))\
                .then_inc(s["wins_set"], 1)
            pool.wait_ge(s["bo_in"], 16)
            pool.wait_ge(s["xrow_ready"], NT)
            pool.tensor_tensor(hb[:, :, :], hrow[:, :, :], bo[:, :].unsqueeze(1).to_broadcast([RT, NT, D]), ALU.add)\
                .then_inc(s["hb_ready"], 1)

            def split_weights(e, slot):
                for m in range(3):
                    if m < 2:
                        src = wraw[:, slot, m, :].rearrange("k (p c) -> k c p", c=HC)
                    else:
                        src = wraw[:, slot, m, :].rearrange("k (c p) -> k c p", c=HC)
                    hi = whi[:, slot, m, :].rearrange("k (c p) -> k c p", c=HC)
                    lo = wlo[:, slot, m, :].rearrange("k (c p) -> k c p", c=HC)
                    if m == 0:
                        pool.tensor_tensor(hi, src, zero[:, 0:1].unsqueeze(2).to_broadcast([128, HC, 128]),
                                           ALU.add).then_inc(s["whi_done"], 1)
                    else:
                        pool.tensor_copy(hi, src).then_inc(s["whi_done"], 1)
                    pool.wait_ge(s["whi_done"], e * 3 + (m + 1))
                    last = pool.tensor_tensor(lo, src, hi, ALU.subtract)
                last.then_inc(s["w_split"], 1)

            def split_columns(e, slot):
                for c in range(N3):
                    pool.wait_ge(s["half_set"], 1)
                    pool.wait_ge(s["xs_done"], e * N3 + (c + 1))
                    pool.tensor_copy(xshi[:, slot, c, :], xs[:, c, :]).then_inc(s["xshi_done"], 1)
                    pool.wait_ge(s["xshi_done"], e * N3 + (c + 1))
                    pool.tensor_tensor(xslo[:, slot, c, :], xs[:, c, :], xshi[:, slot, c, :],
                                       ALU.subtract).then_inc(s["xs_split"], 1)

            pool.wait_ge(w_in[0], 48)
            split_weights(0, 0)

            def low_part(r):
                cols = slice(r * 2 * RT, (r + 1) * 2 * RT)
                pool.wait_ge(s["x2hi_done"], r + 1)
                pool.tensor_tensor(x2lo[:, cols], x2T[:, cols], x2hi[:, cols], ALU.subtract).then_inc(s["x2lo_done"], 1)

            def add_residual(t):
                pool.wait_ge(s["attended_ready"], t + 1)
                pool.tensor_tensor(h2row[:, t, :], attended[:, t % 2, :], hb[:, t, :], ALU.add).then_inc(s["h2_ready"], 1)

            def normalize(t):
                pool.wait_ge(s["mv2_ready"], t + 1)
                pool.tensor_tensor(var2[:, t:t + 1], mv2[:, t, 1:2], eps[:, :], ALU.add).then_inc(s["var2_ready"], 1)
                if t < NT - 3:
                    pool.tensor_tensor(x2row[:, t, :], h2row[:, t, :], mv2[:, t, 0:1].to_broadcast([RT, D]),
                                       ALU.subtract).then_inc(s["centred"], 1)
                pool.wait_ge(s["var2_ready"], t + 1)
                pool.tensor_tensor(rstd2[:, t:t + 1], var2[:, t:t + 1], minus_half[:, t:t + 1], ALU.pow)\
                    .then_inc(s["rstd2_ready"], 1)
                if t < NT - 3:
                    pool.wait_ge(s["centred"], t + 1)
                    pool.wait_ge(s["rstd2_ready"], t + 1)
                    pool.tensor_tensor(x2row[:, t, :], x2row[:, t, :], rstd2[:, t:t + 1].to_broadcast([RT, D]),
                                       ALU.mult).then_inc(s["x2_ready"], 1)

            add_residual(0)
            for t in range(NT):
                if t + 1 < NT:
                    add_residual(t + 1)
                normalize(t)
                if t >= 4 and t % 2 == 0:
                    low_part((t - 4) // 2)
            low_part(4)
            low_part(5)
            pool.wait_ge(w_in[1], 48)
            split_weights(1, 1)
            split_columns(1, 1)
            with pool.Fori(1, E // 2) as pair:
                for slot in range(2):
                    pool.wait_ge(w_in[slot], pair * 48 + 48)
                    pool.wait_ge(s["y_done"], pair * (2 * SE) + (slot - 1) * SE)
                    split_weights(pair * 2 + slot, slot)
                    split_columns(pair * 2 + slot, slot)

        @block.scalar
        def _(act):
            act.dma_start(span_ids[:, :], d["span_ids"]).then_inc(s["spans_in"], 16)
            act.dma_start(bvr[:, :], d["bv"].rearrange("(c p) -> c p", p=128)).then_inc(s["bv_in"], 16)
            act.dma_start(wv[:, :], d["wv"]).then_inc(s["wv_in"], 16)
            act.wait_ge(s["eps_set"], 1)
            act.activation(std1[:, 0:1], eps[:, :], ACT.Sqrt).then_inc(s["act_own"], 1)

            act.wait_ge(s["spec_done"], 1)
            for m in range(2):
                act.activation(sq[:, m, :].rearrange("k (n c) -> k n c", n=N3),
                               ps[m * IM:m * IM + NK, 0:N3, 0:NC3], ACT.Square).then_inc(s["sq_done"], 1)
            act.wait_ge(s["power_ready"], 1)
            act.activation(mag[:, :], power[:, :], ACT.Sqrt).then_inc(s["mag_done"], 1)
            act.wait_ge(s["cnt_saved"], 2)
            act.activation(weight[:, :], cnt1[:, :], ACT.Ln).then_inc(s["ln_done"], 1)
            act.wait_ge(s["act_own"], 1)
            act.activation(std1[:, 0:1], eps[:, :], ACT.Sqrt).then_inc(s["act_own"], 1)

            def save_wvT(g):
                act.wait_ge(s["wvT_done"], g + 1)
                act.activation(wvT[:, 4 * g:4 * g + 4, :], ps[:, WVT_BANKS[g], :].rearrange("p (t n) -> p t n", t=4),
                               ACT.Copy).then_inc(s["wvT_saved"], 1)

            save_wvT(0)
            save_wvT(1)
            for g in range(3):
                act.wait_ge(s["hrow_done"], g + 1)
                act.activation(hrow[:, 4 * g:4 * g + 4, :], ps[0:RT, g, :].rearrange("p (t n) -> p t n", t=4),
                               ACT.Copy).then_inc(s["hrow_saved"], 1)
            act.wait_ge(s["act_own"], 2)
            for g in range(3):
                if g:
                    save_wvT(1 + g)
                act.wait_ge(s["var1_ready"], g + 1)
                act.activation(std1[:, 4 * g:4 * g + 4], mv1[:, 4 * g:4 * g + 4, 1], ACT.Sqrt,
                               bias=eps[:, 0:1]).then_inc(s["std1_ready"], 1)
            for n in range(N3):
                act.wait_ge(s["xT_done"], n + 1)
                act.activation(xT[:, n * NC3:(n + 1) * NC3], ps[:, 3 + n, 0:NC3], ACT.Copy).then_inc(s["xT_saved"], 1)
            act.wait_ge(s["bqk_in"], 32)

            def high_qk(i):
                n, part = PROJECTIONS[i]
                hi = (q_parts + tuple(k_high))[part]
                act.wait_ge(s["qk_done"], i + 1)
                act.activation(hi[:, n * NC3:(n + 1) * NC3], ps[:, QK_BANKS[i], 0:NC3], ACT.Identity,
                               bias=bqk[:, part:part + 1]).then_inc(s["qkhi_done"], 1)

            for i in range(FIRST_QK):
                high_qk(i)
            act.wait_ge(s["lexp_done"], 2)
            act.activation(lexp[:, :], ldot[:, :], ACT.Exp).then_inc(s["lexp_done"], 1)
            for i in range(FIRST_QK, len(PROJECTIONS)):
                high_qk(i)

            def exponentials(t):
                for m in range(2):
                    act.wait_ge(s["nmx_ready"], 2 * t + m + 1)
                    if t >= 2:
                        act.wait_ge(s["difT_done"], t - 1)
                    act.activation(e_m[:, t % 2, m, :], s_m[:, t % 2, m, :], ACT.Exp, bias=nmx[:, t, m:m + 1],
                                   scale=SCALE, accum_out=den[:, t, m:m + 1]).then_inc(s["exp_done"], 1)

            def attend(t):
                act.wait_ge(s["pv_done"], t + 1)
                act.wait_ge(s["dif_ready"], t + 1)
                if t >= 2:
                    act.wait_ge(s["h2_ready"], t - 1)
                act.activation(attended[:, t % 2, :], ps[0:RT, 6, 0:D], ACT.Copy, scale=rden[:, t, 0:1])\
                   .then_inc(s["attended_ready"], 1)

            def save_turned(r):
                act.wait_ge(s["xh_done"], r + 1)
                act.activation(xhT[:, :, r * 2 * RT:(r + 1) * 2 * RT],
                               ps[:, 7, 0:4 * RT].rearrange("p (m c) -> p m c", m=2),
                               ACT.Copy).then_inc(s["xh_saved"], 1)
                cols = slice(r * 2 * RT, (r + 1) * 2 * RT)
                act.wait_ge(s["xh_saved"], r + 1)
                act.activation(x2hi[:, cols], x2T[:, cols], ACT.Copy).then_inc(s["x2hi_done"], 1)

            def route_exponentials(b):
                gs = slice(b * NG // B, (b + 1) * NG // B)
                act.wait_ge(s["lexp2_ready"], b + 1)
                act.activation(pr[:, gs, :], lg[:, gs, :], ACT.Exp).then_inc(s["lexp2_done"], 1)

            exponentials(0)
            for t in range(NT):
                if t >= 2:
                    attend(t - 2)
                if t + 1 < NT:
                    exponentials(t + 1)
                act.wait_ge(s["difT_done"], t + 1)
                if t >= 2:
                    act.wait_ge(s["pv_done"], t - 1)
                act.activation(difT[:, t % 2, :, :], ps[0:RT, 4:6, 0:3 * RT], ACT.Copy).then_inc(s["difT_saved"], 1)
                if t >= 5 and t % 2 and t < NT - 1:
                    save_turned((t - 5) // 2)
            route_exponentials(0)
            attend(NT - 2)
            save_turned(3)
            attend(NT - 1)
            save_turned(4)
            save_turned(5)
            route_exponentials(1)
            act.activation(std1[:, 0:1], eps[:, :], ACT.Silu)

            def silu(step, k, slot=None, bank=None):
                act.wait_ge(s["h1_done"], step + 1)
                act.activation(act_h[k % 2 if slot is None else slot],
                               ps[:, 3 + 2 * (k % 2) if bank is None else bank, 0:NC3], ACT.Silu).then_inc(s["silu_done"], 1)

            def silu_early(i):
                silu(i, i, slot=i, bank=EARLY_BANKS[i % 6])

            def high_columns(n):
                act.wait_ge(s["xs_done"], n + 1)
                act.activation(xshi[:, 0, n, :], xs[:, n, :], ACT.Copy).then_inc(s["xshi_done"], 1)

            act.wait_ge(s["twT_clear"], 1)

            def save_twT(b):
                act.wait_ge(s["twT_done"], b + 1)
                act.activation(twT[0:3 * E, b * CB:(b + 1) * CB], ps[0:3 * E, 6 + b, 0:CB // 2].bitcast(BF16),
                               ACT.Copy).then_inc(s["twT_saved"], 1)

            save_twT(0)
            for i in range(9):
                silu_early(i)
            high_columns(0)
            silu_early(9)
            silu_early(10)
            save_twT(1)
            silu_early(11)

            def high(step, k):
                act.wait_ge(s["gh_done"], step + 1)
                act.activation(ghi[:, k % 3, :], gh[:, k % 3, :], ACT.Copy).then_inc(s["ghi_done"], 1)

            high_columns(1)
            for k in range(2 * SE):
                if k + 1 >= EARLY:
                    silu(k + 1, k + 1)
                high(k, k)
                if k == 0:
                    high_columns(2)
            with act.Fori(1, E // 2 - 1) as pair:
                for k in range(2 * SE):
                    silu(pair * (2 * SE) + (k + 1), k + 1)
                    high(pair * (2 * SE) + k, k)

            def save_picked(g):
                act.wait_ge(s["og_done"], g + 1)
                if g >= 4:
                    act.wait_ge(out_done[g % 4], 16 * (g // 4))
                act.activation(ow[:, g % 4, :, :], ps[:, PICK_BANKS[g], :].rearrange("p (t n) -> p t n", t=4),
                               ACT.Copy).then_inc(s["ow_saved"], 1)

            for k in range(2 * SE):
                if k + 1 < 2 * SE:
                    silu(STEPS - 2 * SE + k + 1, k + 1)
                high(STEPS - 2 * SE + k, k)
                if k == SE + 9:
                    save_picked(0)
                if k == SE + 11:
                    save_picked(1)
            for g in range(2, OT // 4):
                save_picked(g)

        @block.tensor
        def _(pe):
            mm = pe.matmul
            pe.wait_ge(s["dft_ready"], 1)
            pe.wait_ge(s["ohf_ready"], 1)
            for n in range(N3):
                last = mm(ps[0:IM + NK, n, 0:NC3], dft[:, :], oh_frame[:, n * NC3:(n + 1) * NC3], start=True, stop=True)
            last.then_inc(s["spec_done"], 1)
            pe.wait_ge(s["ohs_ready"], 1)
            pe.wait_ge(s["ones_set"], 1)
            for n in range(N3):
                last = mm(ps[0:RT, 3 + n, 0:NC3], ones[:, :], oh_span[:, n * NC3:(n + 1) * NC3],
                          start=True, stop=True)
            last.then_inc(s["cnt_done"], 1)
            pe.wait_ge(s["sel_in"], 16)
            pe.wait_ge(s["bv_in"], 16)
            pe.transpose(ps[:, 6, 0:VC], bvr[:, :], ident[0:VC, 0:VC]).then_inc(s["bvT_done"], 1)

            def turn_wv(g):
                if g == 1:
                    pe.wait_ge(s["bvT_saved"], 1)
                if g >= 2:
                    pe.wait_ge(s["wvT_saved"], g - 1)
                for c in range(4 * g, 4 * g + 4):
                    last = pe.transpose(ps[:, WVT_BANKS[g], (c % 4) * 128:(c % 4 + 1) * 128],
                                        wv[:, c * 128:(c + 1) * 128], ident)
                last.then_inc(s["wvT_done"], 1)

            pe.wait_ge(s["wv_in"], 16)
            turn_wv(0)
            turn_wv(1)
            pe.wait_ge(s["proj_in"], 16)
            pe.wait_ge(s["mag_done"], 1)
            by_id = mag[:, :].rearrange("k (f v) -> k v f", v=V)
            for v in range(V):
                last = mm(ps[0:BF, 0, 0:DS], by_id[:, v, :], projw[:, v, :], start=(v == 0), stop=(v == V - 1))
            last.then_inc(s["enc_done"], 1)
            pe.wait_ge(s["select_ready"], 1)
            pe.wait_ge(s["table_ready"], 1)
            for t in range(NT):
                o, rows = ps[0:RT, t // 4, (t % 4) * D:(t % 4 + 1) * D], select[:, t * RT:(t + 1) * RT]
                mm(o, rows, table_hi, start=True, stop=False)
                last = mm(o, rows, table_lo, start=False, stop=True)
                if t % 4 == 3:
                    last.then_inc(s["hrow_done"], 1)
            turn_wv(2)
            turn_wv(3)
            pe.wait_ge(s["wo_in"], 16)
            pe.wait_ge(s["wvT_saved"], 4)

            def wv_times_wo(chunks):
                for c in chunks:
                    last = mm(ps[:, 7, 0:D], wvT[:, c, :], wo[:, c, :], start=(c == 0), stop=(c == VC - 1))
                return last

            def turn_x(g):
                pe.wait_ge(s["xrow_ready"], 4 * g + 4)
                for t in range(4 * g, 4 * g + 4):
                    last = pe.transpose(ps[:, 3 + g, (t % 4) * RT:(t % 4 + 1) * RT], xrow[:, t, :], ident[0:RT, 0:RT])
                last.then_inc(s["xT_done"], 1)

            wv_times_wo(range(VC // 2))
            pe.wait_ge(s["cnt_saved"], 2)
            turn_x(0)
            wv_times_wo(range(VC // 2, VC)).then_inc(s["wvo_done"], 1)
            pe.wait_ge(s["onesf_set"], 1)
            pe.wait_ge(s["pool_own"], 5)
            mm(ps[0:RT, 6, 0:D], ones_f[:, :], bvw[:, 0, :], start=True, stop=True).then_inc(s["bvob_done"], 1)
            turn_x(1)
            turn_x(2)
            pe.wait_ge(s["wqkv_in"], 32)

            def project(i):
                n, part = PROJECTIONS[i]
                pe.wait_ge(s["xT_saved"], 1 if i < 4 else N3)
                if i == 0:
                    pe.wait_ge(s["hrow_saved"], 3)
                if QK_BANKS[i] in QK_BANKS[:i]:
                    pe.wait_ge(s["qklo_done"], QK_BANKS.index(QK_BANKS[i]) + 1)
                if QK_BANKS[i] == 6:
                    pe.wait_ge(s["bvo_saved"], 1)
                if QK_BANKS[i] == 7:
                    pe.wait_ge(s["wvo_saved"], 1)
                mm(ps[:, QK_BANKS[i], 0:NC3], wqkv[:, part, :, :].rearrange("k a n -> k (a n)"),
                   xT[:, n * NC3:(n + 1) * NC3], start=True, stop=True).then_inc(s["qk_done"], 1)

            for i in range(FIRST_QK):
                project(i)

            def values(g):
                pe.wait_ge(s["qklo_done"], len(PROJECTIONS))
                if g == 2:
                    pe.wait_ge(s["vw_saved"], 1)
                for t in range(4 * g, 4 * g + 4):
                    last = mm(ps[0:RT, VW_BANKS[g], (t % 4) * D:(t % 4 + 1) * D], xT[:, t * RT:(t + 1) * RT],
                              wvo[:, :], start=True, stop=True)
                last.then_inc(s["vw_done"], 1)

            def scores(t):
                b = t // TB
                for m in range(2):
                    if t >= 1:
                        pe.wait_ge(s["sc_saved"], 2 * t - 1 + m)
                    rows = slice(t * RT, (t + 1) * RT)
                    for j in range(2):
                        keys = slice(b * CB + j * KH, b * CB + (j + 1) * KH)
                        o = ps[0:RT, 2 * m + j, 0:KH]
                        mm(o, q_parts[m][:, rows], k_high[m][:, keys], start=True, stop=False)
                        last = mm(o, q_parts[m][:, rows], k_low[m][:, keys], start=False, stop=True)
                    last.then_inc(s["sc_done"], 1)

            def turn_back(r):
                if r >= 1:
                    pe.wait_ge(s["xh_saved"], r)
                pe.wait_ge(s["x2_ready"], 2 * r + 2)
                for i, rows in enumerate((x2row, h2row)):
                    for u in range(2):
                        last = pe.transpose(ps[:, 7, (2 * i + u) * RT:(2 * i + u + 1) * RT], rows[:, 2 * r + u, :],
                                            ident[0:RT, 0:RT])
                last.then_inc(s["xh_done"], 1)

            def logits(r):
                pe.wait_ge(s["router_in"], 32)
                pe.wait_ge(s["xh_saved"], r + 1)
                pe.wait_ge(s["attended_ready"], NT if r >= 3 else 2 * r + 5)
                for t in (2 * r, 2 * r + 1):
                    last = mm(ps[0:RT, 6, 256 + t * (G + E):256 + (t + 1) * (G + E)], x2T[:, t * RT:(t + 1) * RT], wrg[:, :],
                              start=True, stop=True)
                last.then_inc(s["logit_done"], 1)

            def times_values(t):
                pe.wait_ge(s["difT_saved"], t + 1)
                pe.wait_ge(s["vw_saved"], 3 if t else 2)
                if t >= 1:
                    pe.wait_ge(s["attended_ready"], t)
                if t >= 5 and t % 2 and t < NT - 1:
                    logits((t - 5) // 2)
                for j in range(TB):
                    last = mm(ps[0:RT, 6, 0:D], difT[:, t % 2, j // 3, (j % 3) * RT:(j % 3 + 1) * RT], vw[:, (t // TB) * TB + j, :],
                              start=(j == 0), stop=(j == TB - 1))
                last.then_inc(s["pv_done"], 1)

            pe.wait_ge(s["qklo_done"], 8)
            scores(0)
            for i in range(FIRST_QK, len(PROJECTIONS)):
                project(i)
            scores(1)
            values(0)
            values(1)
            for t in range(NT):
                if t >= 2:
                    times_values(t - 2)
                if t + 2 < NT:
                    scores(t + 2)
                if t >= 1:
                    pe.wait_ge(s["difT_saved"], t)
                pe.wait_ge(s["dif_ready"], t + 1)
                for j in range(TB):
                    last = pe.transpose(ps[0:RT, 4 + j // 3, (j % 3) * RT:(j % 3 + 1) * RT],
                                        e_m[:, t % 2, 0, j * RT:(j + 1) * RT], ident[0:RT, 0:RT])
                last.then_inc(s["difT_done"], 1)
                if t == 0:
                    values(2)
                if t >= 5 and t % 2 and t < NT - 1:
                    turn_back((t - 5) // 2)

            def place(step, k, last):
                slot, r = divmod(k % (2 * SE), SE)
                if (isinstance(step, int) and step < SE) or (last and slot == 1):
                    return slot, r % HC, r // HC
                return slot, r // N3, r % N3

            def times_w1(step, k, e, last=False, bank=None):
                slot, j, n = place(step, k, last)
                if k % SE == 0:
                    pe.wait_ge(s["w_split"], e + 1)
                c = slice(j * 128, (j + 1) * 128)
                cols = slice(n * NC3, (n + 1) * NC3)
                o = ps[:, 3 + 2 * (k % 2) if bank is None else bank, 0:NC3]
                mm(o, whi[:, slot, 0, c], x2hi[:, cols], start=True, stop=False)
                mm(o, wlo[:, slot, 0, c], x2hi[:, cols], start=False, stop=False)
                mm(o, whi[:, slot, 0, c], x2lo[:, cols], start=False, stop=True).then_inc(s["h1_done"], 1)

            def early(i):
                if i >= 6:
                    pe.wait_ge(s["silu_done"], i - 5)
                pe.wait_ge(s["x2lo_done"], (2, 4, NT // 2)[i // HC])
                times_w1(i, i, 0, bank=EARLY_BANKS[i % 6])

            pe.wait_ge(s["logit_saved"], 1)
            times_values(NT - 2)
            turn_back(3)
            times_values(NT - 1)
            turn_back(4)
            logits(3)
            pe.wait_ge(s["sc_saved"], 2 * NT)
            pe.wait_ge(s["difT_saved"], NT)
            for i in range(IN_TURNING):
                early(i)
            turn_back(5)
            logits(4)
            logits(5)
            for i in range(IN_TURNING, 6):
                early(i)

            def spread(e, n):
                mm(ps[:, 7, 0:NC3], rep[:, bass.ds(e, 1), :].rearrange("k a n -> k (a n)"), twT[:, n * NC3:(n + 1) * NC3],
                   start=True, stop=True).then_inc(s["tws_done"], 1)

            pe.wait_ge(s["id16_ready"], 1)
            pe.wait_ge(s["logit_saved"], B)

            def turn_tw(b):
                pe.wait_ge(s["tw_ready"], b + 1)
                for t in range(b * TB, (b + 1) * TB):
                    last = pe.transpose(ps[0:3 * E, 6 + b, 0:CB // 2].bitcast(BF16)[:, (t % TB) * RT:(t % TB + 1) * RT],
                                        tw3[:, t, :], ident16[0:RT, 0:RT])
                last.then_inc(s["twT_done"], 1)

            turn_tw(0)
            early(6)
            pe.wait_ge(s["twT_saved"], 1)
            pe.wait_ge(s["rep_ready"], 1)
            spread(0, 0)
            for i in range(7, 11):
                early(i)
            pe.wait_ge(s["xs_done"], 1)
            turn_tw(1)
            early(11)

            def hidden(step, k, e, last=False):
                slot, j, n = place(step, k, last)
                if not (isinstance(step, int) and step < 2):
                    pe.wait_ge(s["gh_done"], step - 1)
                if not (isinstance(step, int) and step < EARLY):
                    times_w1(step, k, e, last)
                c = slice(j * 128, (j + 1) * 128)
                if j == 0:
                    pe.wait_ge(s["xs_split"], e * N3 + (n + 1))
                o = ps[:, 4 + 2 * (k % 2), 0:NC3]
                mm(o, whi[:, slot, 1, c], xshi[:, slot, n, :], start=True, stop=False)
                mm(o, wlo[:, slot, 1, c], xshi[:, slot, n, :], start=False, stop=False)
                mm(o, whi[:, slot, 1, c], xslo[:, slot, n, :], start=False, stop=True).then_inc(s["h3_done"], 1)

            def back(step, k, last):
                slot, j, n = place(step, k, last)
                c = slice(j * 128, (j + 1) * 128)
                o = ps[:, n, 0:NC3]
                pe.wait_ge(s["ghi_done"], step + 1)
                first = isinstance(step, int) and step < SE and j == 0
                mm(o, whi[:, slot, 2, c], ghi[:, k % 3, :], start=first, stop=False, skip_group_check=True)
                mm(o, wlo[:, slot, 2, c], ghi[:, k % 3, :], start=False, stop=False, skip_group_check=True)
                pe.wait_ge(s["glo_done"], step + 1)
                mm(o, whi[:, slot, 2, c], glo[:, k % 3, :], start=False, stop=True,
                   skip_group_check=True).then_inc(s["y_done"], 1)

            def windows(g):
                before = [q for q in range(g) if WINDOW_BANKS[q] == WINDOW_BANKS[g]]
                if before:
                    pe.wait_ge(s["yw_saved"], before[-1] + 1)
                else:
                    pe.wait_ge(s["xs_done"], E * N3)
                tiles = range(4 * g, 4 * g + 4)
                starts = [t // (OT // B) * CB + 2 * V * (t % (OT // B)) for t in tiles]
                pe.wait_ge(s["y_saved"], -(-(starts[-1] + WIN) // NC3))
                for t, at in enumerate(starts):
                    last = pe.transpose(ps[0:WIN, WINDOW_BANKS[g], t * D:(t + 1) * D], yT[:, at:at + WIN], ident)
                last.then_inc(s["yw_done"], 1)

            def picks(g):
                before = [q for q in range(g) if PICK_BANKS[q] == PICK_BANKS[g]]
                if before:
                    pe.wait_ge(s["ow_saved"], before[-1] + 1)
                elif g:
                    pe.wait_ge(s["gh_done"], STEPS)
                pe.wait_ge(s["yw_saved"], g + 1)
                for t in range(4):
                    tile = 4 * g + t
                    last = mm(ps[:, PICK_BANKS[g], t * D:(t + 1) * D], oh_out[:, tile * 128:(tile + 1) * 128],
                              yw[:, g % 2, t, :], start=True, stop=True)
                last.then_inc(s["og_done"], 1)

            def pair_steps(base, e0, last):
                for k in range(2 * SE):
                    if k + 2 < 2 * SE or not last:
                        hidden(base + (k + 2), k + 2, e0 + (k + 2) // SE, last)
                    back(base + k, k, last)
                    e_in, r = divmod(k, SE)
                    if r in (1, 3, 5) and not (last and e_in == 1):
                        n = (r - 1) // 2
                        pe.wait_ge(s["xs_done"], (e0 + (e_in + 1)) * N3 + n)
                        spread(e0 + (e_in + 1), n)
                    if last:
                        if k == SE + 6:
                            windows(0)
                        if k == SE + 8:
                            windows(1)
                            pe.wait_ge(s["oh_done"], OHC)
                            picks(0)
                        if k == SE + 10:
                            windows(2)
                            picks(1)
                        if k == SE + 11:
                            windows(3)

            pe.wait_ge(s["twT_saved"], B)
            spread(0, 1)
            hidden(0, 0, 0)
            pe.wait_ge(s["xs_done"], 2)
            spread(0, 2)
            hidden(1, 1, 0)
            pair_steps(0, 0, False)
            with pe.Fori(1, E // 2 - 1) as pair:
                pair_steps(pair * (2 * SE), pair * 2, False)
            pair_steps(STEPS - 2 * SE, E - 2, True)

            for g in range(2, OT // 4):
                picks(g)
                if g + 2 < OT // 4:
                    windows(g + 2)

        @block.vector
        def _(dve):
            made = [0]

            def link(ins):
                made[0] += 1
                ins.then_inc(s["own"], 1)
                dve.wait_ge(s["own"], made[0])

            dve.wait_ge(s["ids_in"], 16)
            link(dve.tensor_copy(frame_f[:, :], frame_ids[:, :]))
            dve.wait_ge(s["early_in"], 16)
            vid = kc[:, K_VID:K_VID + V].unsqueeze(1)
            dve.tensor_tensor(oh_frame[:, :].rearrange("n (f v) -> n f v", v=V),
                              frame_f[:, :].unsqueeze(2).to_broadcast([2 * HOP, BF, V]),
                              vid.to_broadcast([2 * HOP, BF, V]), ALU.is_equal).then_inc(s["ohf_ready"], 1)
            dve.wait_ge(s["spans_in"], 16)
            link(dve.tensor_tensor(span_f[:, :], span_ids[:, :], kc[0:SPAN, K_PAD:K_PAD + BF], ALU.add))
            dve.tensor_tensor(oh_span[:, :].rearrange("n (f v) -> n f v", v=V),
                              span_f[:, :].unsqueeze(2).to_broadcast([SPAN, BF, V]),
                              vid[0:SPAN].to_broadcast([SPAN, BF, V]), ALU.is_equal).then_inc(s["ohs_ready"], 1)
            dve.wait_ge(s["bvT_done"], 1)
            dve.tensor_copy(bvT[:, :], ps[:, 6, 0:VC]).then_inc(s["bvT_saved"], 1)
            dve.wait_ge(s["sq_done"], 2)
            dve.tensor_tensor(power[:, :], sq[:, 0, :], sq[:, 1, :], ALU.add).then_inc(s["power_ready"], 1)
            dve.wait_ge(s["cnt_done"], 1)
            counts = ps[0:RT, 3:6, 0:NC3]
            dve.tensor_scalar(cnt1[:, :].rearrange("p (n c) -> p n c", n=N3), counts, 1.0, None, ALU.max)\
               .then_inc(s["cnt_saved"], 1)
            dve.tensor_scalar(absent[:, :].rearrange("p (n c) -> p n c", n=N3), counts, 0.0, NEG, ALU.is_equal, ALU.mult)\
               .then_inc(s["cnt_saved"], 1)
            dve.wait_ge(s["enc_done"], 1)
            dve.wait_ge(s["projb_in"], 16)
            dve.wait_ge(s["table_clear"], 1)
            link(dve.tensor_tensor(table[0:BF, DE:D], ps[0:BF, 0, 0:DS], projb[:, :], ALU.add))
            dve.wait_ge(s["emb_in"], 16)
            dve.tensor_copy(table_hi, table[:, :]).then_inc(s["table_high"], 1)
            dve.wait_ge(s["table_high"], 1)
            dve.tensor_tensor(table_lo, table[:, :], table_hi, ALU.subtract).then_inc(s["table_ready"], 1)

            def h_statistics(g):
                dve.wait_ge(s["hrow_saved"], g + 1)
                for t in range(4 * g, 4 * g + 4):
                    last = dve.bn_stats(st1[:, t, :], hrow[:, t, :])
                link(last)
                for t in range(4 * g, 4 * g + 4):
                    last = dve.bn_aggr(mv1[:, t, :], st1[:, t, :])
                last.then_inc(s["var1_ready"], 1)

            def h_normalize(g):
                dve.wait_ge(s["std1_ready"], g + 1)
                link(dve.reciprocal(rstd1[:, 4 * g:4 * g + 4], std1[:, 4 * g:4 * g + 4]))
                for t in range(4 * g, 4 * g + 4):
                    dve.tensor_scalar(xrow[:, t, :], hrow[:, t, :], mv1[:, t, 0:1], rstd1[:, t:t + 1],
                                      ALU.subtract, ALU.mult).then_inc(s["xrow_ready"], 1)

            h_statistics(0)
            h_statistics(1)
            h_normalize(0)
            h_statistics(2)
            h_normalize(1)
            h_normalize(2)
            dve.wait_ge(s["lam_in"], 64)
            for i in range(2):
                dve.tensor_tensor_reduce(out=ljunk[:, i, :], in0=lqk[:, 2 * i, :], in1=lqk[:, 2 * i + 1, :], scale=1.0,
                                         scalar=0.0, op0=ALU.mult, op1=ALU.add,
                                         accum_out=ldot[:, i:i + 1]).then_inc(s["lexp_done"], 1)
            dve.wait_ge(s["wvo_done"], 1)
            dve.tensor_copy(wvo[:, :], ps[:, 7, 0:D]).then_inc(s["wvo_saved"], 1)
            dve.wait_ge(s["bvob_done"], 1)
            dve.tensor_copy(bvo[:, :], ps[0:RT, 6, 0:D]).then_inc(s["bvo_saved"], 1)
            dve.wait_ge(s["ln_done"], 1)
            link(dve.scalar_tensor_tensor(out=weight[:, :], in0=weight[:, :], scalar=1.0 / SCALE, in1=absent[:, :],
                                          op0=ALU.mult, op1=ALU.add))

            def low_qk(i):
                n, part = PROJECTIONS[i]
                cols = slice(n * NC3, (n + 1) * NC3)
                rows = slice(QD, 128) if part < 2 else slice(0, 128)
                hi = (q_parts + tuple(k_high))[part]
                lo = (q_parts + tuple(k_low))[part]
                dve.wait_ge(s["qkhi_done"], i + 1)
                dve.scalar_tensor_tensor(out=lo[rows, cols], in0=ps[rows, QK_BANKS[i], 0:NC3],
                                         scalar=bqk[rows, part:part + 1], in1=hi[rows, cols],
                                         op0=ALU.add, op1=ALU.subtract).then_inc(s["qklo_done"], 1)

            for i in range(FIRST_QK):
                low_qk(i)

            def weigh_max(t):
                b = t // TB
                keys = slice(b * CB, (b + 1) * CB)
                for m in range(2):
                    dve.wait_ge(s["sc_done"], 2 * t + m + 1)
                    if t >= 2:
                        dve.wait_ge(s["exp_done"], 2 * t - 3 + m)
                    dve.tensor_tensor_reduce(out=s_m[:, t % 2, m, :].rearrange("p (j c) -> p j c", j=2),
                                             in0=ps[0:RT, 2 * m:2 * m + 2, 0:KH],
                                             in1=weight[:, keys].rearrange("p (j c) -> p j c", j=2),
                                             scale=1.0, scalar=-3.0e38, op0=ALU.add, op1=ALU.max,
                                             accum_out=mx[:, t, m:m + 1]).then_inc(s["sc_saved"], 1)
                for m in range(2):
                    dve.wait_ge(s["sc_saved"], 2 * t + m + 1)
                    dve.tensor_scalar(nmx[:, t, m:m + 1], mx[:, t, m:m + 1], -SCALE, None, ALU.mult)\
                       .then_inc(s["nmx_ready"], 1)

            def difference(t):
                dve.wait_ge(s["exp_done"], 2 * t + 2)
                link(dve.reciprocal(rden[:, t, :], den[:, t, :]))
                link(dve.scalar_tensor_tensor(out=ratio[:, t:t + 1], in0=den[:, t, 0:1], scalar=neglam[:, 0:1],
                                              in1=rden[:, t, 1:2], op0=ALU.mult, op1=ALU.mult))
                dve.scalar_tensor_tensor(out=e_m[:, t % 2, 0, :], in0=e_m[:, t % 2, 1, :], scalar=ratio[:, t:t + 1],
                                         in1=e_m[:, t % 2, 0, :], op0=ALU.mult, op1=ALU.add).then_inc(s["dif_ready"], 1)

            def statistics(t):
                dve.wait_ge(s["h2_ready"], t + 1)
                link(dve.bn_stats(st2[:, t, :], h2row[:, t, :]))
                dve.bn_aggr(mv2[:, t, :], st2[:, t, :]).then_inc(s["mv2_ready"], 1)

            def normalize(t):
                dve.wait_ge(s["rstd2_ready"], t + 1)
                dve.tensor_scalar(x2row[:, t, :], h2row[:, t, :], mv2[:, t, 0:1], rstd2[:, t:t + 1],
                                  ALU.subtract, ALU.mult).then_inc(s["x2_ready"], 1)

            def route_scores(b):
                gs = slice(b * NG // B, (b + 1) * NG // B)
                S3 = [RT, NG // B, 4]
                dve.wait_ge(s["logit_done"], (b + 1) * NT // 2 // B)
                dve.wait_ge(s["attended_ready"], NT if b == B - 1 else NT - 2)
                dve.wait_ge(s["rbias_in"], 32)
                by_tile = lg[:, gs, :].rearrange("p (t a) e -> p t (a e)", t=TB)
                at = 256 + b * TB * (G + E)
                dve.tensor_tensor(by_tile, ps[0:RT, 6, at:at + TB * (G + E)].rearrange("p (t a) -> p t a", t=TB),
                                  brg[:, :].unsqueeze(1).to_broadcast([RT, TB, G + E]), ALU.add).then_inc(s["logit_saved"], 1)
                dve.wait_ge(s["logit_saved"], b + 1)
                link(dve.tensor_reduce(lmx[:, gs], lg[:, gs, :], X, ALU.max))
                dve.tensor_tensor(lg[:, gs, :], lg[:, gs, :], lmx[:, gs].unsqueeze(2).to_broadcast(S3),
                                  ALU.subtract).then_inc(s["lexp2_ready"], 1)

            def route_compare(b):
                gs = slice(b * NG // B, (b + 1) * NG // B)
                S3 = [RT, NG // B, 4]
                dve.wait_ge(s["wins_set"], 1)
                dve.wait_ge(s["lexp2_done"], b + 1)
                link(dve.tensor_reduce(lsum[:, gs], pr[:, gs, :], X, ALU.add))
                link(dve.reciprocal(lsum[:, gs], lsum[:, gs]))
                link(dve.tensor_tensor(pr[:, gs, :], pr[:, gs, :], lsum[:, gs].unsqueeze(2).to_broadcast(S3), ALU.mult))
                for w, off in wins:
                    last = dve.tensor_tensor(w[:, gs, off:4], pr[:, gs, 0:4 - off], pr[:, gs, off:4], ALU.is_ge)
                link(last)
                for (w, off), o in zip(wins, (rank, part2, part3)):
                    last = dve.tensor_tensor(o[:, gs, :], w[:, gs, 0:4], w[:, gs, off:off + 4], ALU.subtract)
                link(last)

            def route_rank(b):
                gs = slice(b * NG // B, (b + 1) * NG // B)
                link(dve.tensor_tensor(rank[:, gs, :], rank[:, gs, :], part2[:, gs, :], ALU.add))
                link(dve.tensor_tensor(rank[:, gs, :], rank[:, gs, :], part3[:, gs, :], ALU.add))
                dve.scalar_tensor_tensor(out=top1[:, gs, :], in0=rank[:, gs, :], scalar=0.0, in1=pr[:, gs, :],
                                         op0=ALU.is_equal, op1=ALU.mult)
                link(dve.scalar_tensor_tensor(out=top2[:, gs, :], in0=rank[:, gs, :], scalar=1.0, in1=pr[:, gs, :],
                                              op0=ALU.is_equal, op1=ALU.mult))
                dve.tensor_reduce(p1[:, gs], top1[:, gs, :], X, ALU.add)
                link(dve.tensor_reduce(p2[:, gs], top2[:, gs, :], X, ALU.add))

            def route_second(b):
                gs = slice(b * NG // B, (b + 1) * NG // B)
                link(dve.tensor_tensor(keep2[:, gs], p1[:, gs], p2[:, gs], ALU.add))
                link(dve.tensor_scalar(keep2[:, gs], keep2[:, gs], 0.9, None, ALU.is_le))
                link(dve.tensor_tensor(p2[:, gs], p2[:, gs], keep2[:, gs], ALU.mult))

            def route_shares(b):
                gs = slice(b * NG // B, (b + 1) * NG // B)
                S3 = [RT, NG // B, 4]
                dve.tensor_tensor(top2[:, gs, :], top2[:, gs, :], keep2[:, gs].unsqueeze(2).to_broadcast(S3), ALU.mult)
                link(dve.scalar_tensor_tensor(out=p1[:, gs], in0=p1[:, gs], scalar=1e-9, in1=p2[:, gs], op0=ALU.add, op1=ALU.add))
                link(dve.reciprocal(p1[:, gs], p1[:, gs]))
                link(dve.tensor_tensor(rn[:, gs, :], top1[:, gs, :], top2[:, gs, :], ALU.add))
                link(dve.tensor_tensor(rn[:, gs, :], rn[:, gs, :], p1[:, gs].unsqueeze(2).to_broadcast(S3), ALU.mult))

            def route_weights(b):
                gs = slice(b * NG // B, (b + 1) * NG // B)
                ts = slice(b * TB, (b + 1) * TB)
                of = rn[:, gs, :].rearrange("p (t a) e -> p t a e", t=TB)
                link(dve.tensor_scalar(rn[:, gs, :].rearrange("p (t a) e -> p t a e", t=TB)[:, :, 0, :], of[:, :, 0, :],
                                       float(G) ** -0.5, None, ALU.mult))
                tw4 = tw[:, ts, :].rearrange("p t (g e) -> p t g e", g=G)
                link(dve.tensor_tensor(tw4, of[:, :, 1:, :], of[:, :, 0, :].unsqueeze(3).to_broadcast([RT, TB, G, EPG]), ALU.mult))
                for part in range(3):
                    o = tw3[:, ts, part * E:(part + 1) * E]
                    ins = dve.tensor_copy(o, tw[:, ts, :])
                    if part < 2:
                        link(ins)
                        link(dve.tensor_tensor(tw[:, ts, :], tw[:, ts, :], o, ALU.subtract))
                    else:
                        ins.then_inc(s["tw_ready"], 1)

            def scale_columns(e, n):
                dve.wait_ge(s["tws_done"], e * N3 + (n + 1))
                if not (isinstance(e, int) and e == 0):
                    dve.wait_ge(s["xs_split"], (e - 1) * N3 + (n + 1))
                dve.tensor_tensor(xs[:, n, :], x2T[:, n * NC3:(n + 1) * NC3], ps[:, 7, 0:NC3],
                                  ALU.mult).then_inc(s["xs_done"], 1)

            weigh_max(0)
            for i in range(FIRST_QK, len(PROJECTIONS)):
                low_qk(i)
            for t in range(NT):
                if t + 1 < NT:
                    weigh_max(t + 1)
                if t == 0:
                    dve.wait_ge(s["lexp_done"], 3)
                    link(dve.tensor_tensor(neglam[:, :], lexp[:, 1:2], lexp[:, 0:1], ALU.subtract))
                    link(dve.tensor_scalar(neglam[:, :], neglam[:, :], -LAM0, None, ALU.add))
                difference(t)
                for g in ((0, 1), (2,), ())[min(t, 2)]:
                    dve.wait_ge(s["bvo_saved"], 1)
                    dve.wait_ge(s["vw_done"], g + 1)
                    dve.tensor_tensor(vw[:, 4 * g:4 * g + 4, :], ps[0:RT, VW_BANKS[g], :].rearrange("p (t n) -> p t n", t=4),
                                      bvo[:, :].unsqueeze(1).to_broadcast([RT, 4, D]), ALU.add).then_inc(s["vw_saved"], 1)
                if t >= 3:
                    statistics(t - 3)
            route_scores(0)
            statistics(NT - 3)
            route_compare(0)
            statistics(NT - 2)
            normalize(NT - 3)
            route_rank(0)
            statistics(NT - 1)
            normalize(NT - 2)
            route_second(0)
            normalize(NT - 1)
            route_shares(0)
            route_weights(0)
            route_scores(1)
            route_compare(1)
            route_rank(1)
            route_second(1)
            scale_columns(0, 0)
            route_shares(1)
            route_weights(1)

            def gate(step, k, slot=None):
                dve.wait_ge(s["silu_done"], step + 1 if slot is None else slot + 1)
                dve.wait_ge(s["h3_done"], step + 1)
                dve.tensor_tensor(gh[:, k % 3, :], act_h[k % 2 if slot is None else slot], ps[:, 4 + 2 * (k % 2), 0:NC3],
                                  ALU.mult).then_inc(s["gh_done"], 1)

            def low(step, k):
                dve.wait_ge(s["ghi_done"], step + 1)
                dve.tensor_tensor(glo[:, k % 3, :], gh[:, k % 3, :], ghi[:, k % 3, :],
                                  ALU.subtract).then_inc(s["glo_done"], 1)

            def save_sums(n):
                dve.wait_ge(s["y_done"], STEPS - (N3 - 1 - n) * HC)
                cols = slice(n * NC3, (n + 1) * NC3)
                dve.tensor_tensor(yT[:, cols], ps[:, n, 0:NC3], h2T[:, cols], ALU.add).then_inc(s["y_saved"], 1)

            def save_windows(g):
                dve.wait_ge(s["yw_done"], g + 1)
                if g >= 2:
                    dve.wait_ge(s["og_done"], g - 1)
                dve.tensor_copy(yw[:, g % 2, :, :], ps[0:WIN, WINDOW_BANKS[g], :].rearrange("p (t n) -> p t n", t=4))\
                   .then_inc(s["yw_saved"], 1)

            def pair_steps(base, e0, last):
                for k in range(2 * SE):
                    if k + 1 < 2 * SE or not last:
                        early = isinstance(base, int) and base + k + 1 < EARLY
                        gate(base + (k + 1), k + 1, slot=k + 1 if early else None)
                    low(base + k, k)
                    e_in, r = divmod(k, SE)
                    if r in (2, 4, 6) and not (last and e_in == 1):
                        scale_columns(e0 + (e_in + 1), (r - 2) // 2)
                    if isinstance(base, int) and base == 0 and k == 1:
                        low_columns(2)
                    if last and k < OHC:
                        pick_classes(k)
                    if last:
                        if k == SE + 5:
                            save_sums(0)
                        if k == SE + 7:
                            save_windows(0)
                        if k == SE + 9:
                            save_sums(1)
                            save_windows(1)
                        if k == SE + 11:
                            save_windows(2)

            def pick_classes(i):
                at = i * (B * L // OHC)
                dve.tensor_tensor(oh_out[:, at:at + B * L // OHC], ids_wide[:, at:at + B * L // OHC],
                                  pick[:, at % L:at % L + B * L // OHC], ALU.is_equal).then_inc(s["oh_done"], 1)

            def low_columns(n):
                dve.wait_ge(s["xshi_done"], n + 1)
                dve.tensor_tensor(xslo[:, 0, n, :], xs[:, n, :], xshi[:, 0, n, :], ALU.subtract).then_inc(s["xs_split"], 1)

            dve.wait_ge(s["pick_in"], 16)
            dve.wait_ge(s["idswide_in"], 16)
            low_columns(0)
            scale_columns(0, 1)
            gate(0, 0, slot=0)
            low_columns(1)
            scale_columns(0, 2)
            pair_steps(0, 0, False)
            with dve.Fori(1, E // 2 - 1) as pair:
                pair_steps(pair * (2 * SE), pair * 2, False)
            pair_steps(STEPS - 2 * SE, E - 2, True)
            save_sums(2)
            for g in range(3, OT // 4):
                save_windows(g)


_INS = {
    "emb": "L0_tok_emb_table", "proj_w": "L0_tok_proj_w", "proj_b": "L0_tok_proj_b", "wqkv": "L0_attn_Wqkv",
    "bqkv": "L0_attn_bqkv", "wv": "L0_attn_Wv", "bv": "L0_attn_bv", "wo": "L0_attn_Wo", "bo": "L0_attn_bo",
    "lq1": "L0_attn_lq1", "lk1": "L0_attn_lk1", "lq2": "L0_attn_lq2", "lk2": "L0_attn_lk2", "wr": "L0_ffn_Wr",
    "br": "L0_ffn_br", "wgate": "L0_ffn_Wgate", "bgate": "L0_ffn_bgate", "w1": "L0_ffn_W1", "w3": "L0_ffn_W3",
    "w2": "L0_ffn_W2",
}


def kernel(**inputs):
    import concourse.bacc as _bacc
    from concourse.bass_utils import run_bass_kernel_spmd as _run

    ids = np.ascontiguousarray(inputs["x"])
    packed, pick = shape_constants()
    span_at, _ = bucket_index()
    laid = {n: np.ascontiguousarray(inputs[full]) for n, full in _INS.items()}
    laid["ids"] = ids
    frames = ids[:, frame_index()].reshape(BF, HOP).T
    laid["frame_ids"] = np.concatenate([frames, frames])
    laid["span_ids"] = np.ascontiguousarray(ids[:, span_at].reshape(BF, SPAN).T)
    laid["kc"] = packed
    laid["pick"] = pick

    nc = _bacc.Bacc("TRN2", target_bir_lowering=False, num_devices=1)
    arrays, d = {}, {}
    for n, a in laid.items():
        arrays[f"in_{n}_dram"] = a
        d[n] = nc.dram_tensor(f"in_{n}_dram", a.shape, mybir.dt.from_np(a.dtype), kind="ExternalInput").ap()
    out = nc.dram_tensor("out_dram", (B, L, D), F32, kind="ExternalOutput").ap()
    build(nc, d, out)
    r = _run(nc, [arrays], core_ids=[0])
    return r.results[0]["out_dram"]
```
